# Optimizing a Trainium2 kernel written in Bass

```python
import numpy as np
import jax
import jax.numpy as jnp

def _softmax(x, axis=-1):
    return jax.nn.softmax(x, axis=axis)

def _gelu(x):
    return jax.nn.gelu(x, approximate=True)

def _silu(x):
    return jax.nn.silu(x)

def _sigmoid(x):
    return jax.nn.sigmoid(x)

def _layernorm(x, axis=-1, eps=1e-05):
    m = jnp.mean(x, axis=axis, keepdims=True)
    v = jnp.var(x, axis=axis, keepdims=True)
    return (x - m) / jnp.sqrt(v + eps)

def _scatter_add(tgt, idx, src, axis=0):
    return tgt.at[idx].add(src)

def _segment_sum(src, seg, n):
    return jax.ops.segment_sum(src, seg, n)
kernel_name = 'mk_adj_preln_d2_adj_r2_b048bf'

def setup_inputs(seed: int=0):
    np.random.seed(seed)
    _w = jnp.asarray

    def _rec_inputs():
        import jax
        import jax.numpy as jnp
        _gk = jax.random.key(seed)
        x = -0.0002928 + 1 * jax.random.normal(jax.random.fold_in(_gk, 1), (2048, 256), jnp.float32)
        _a = jax.random.bernoulli(jax.random.fold_in(_gk, 2), 0.000976562, (2048, 2048))
        _a = jnp.logical_or(_a, jnp.swapaxes(_a, -1, -2))
        _a = jnp.logical_or(_a, jnp.eye(2048, dtype=bool))
        _af = _a.astype(jnp.float32)
        _af = _af * jax.random.uniform(jax.random.fold_in(_gk, 3), (2048, 2048), jnp.float32, 0.05, 0.00012207)
        adj = _af
        return (x, adj)
    x, adj = _rec_inputs()

    def _L0_gnn_setup():
        import jax, jax.numpy as jnp
        import numpy as np
        N = 4096
        INPUT_DIM = 256
        HIDDEN_DIM = 128

        def gcn_layer(adj, x, w):
            return jax.nn.relu(adj @ (x @ w))
        key = jax.random.key(seed)
        ks = jax.random.split(key, 8)
        scale = 0.05
        X = jax.random.normal(ks[0], (N, INPUT_DIM), dtype=jnp.float32)
        adj_ = jax.random.uniform(ks[1], (N, N), dtype=jnp.float32) / N
        dims = [(INPUT_DIM, HIDDEN_DIM), (HIDDEN_DIM, HIDDEN_DIM), (HIDDEN_DIM, HIDDEN_DIM // 2), (HIDDEN_DIM // 2, HIDDEN_DIM), (HIDDEN_DIM, HIDDEN_DIM), (HIDDEN_DIM, INPUT_DIM)]
        Ws = [jax.random.normal(ks[2 + i], d, dtype=jnp.float32) * scale for i, d in enumerate(dims)]
        return {'X': X, 'adj_': adj_, 'W1': Ws[0], 'W2': Ws[1], 'W3': Ws[2], 'W4': Ws[3], 'W5': Ws[4], 'W6': Ws[5]}
    _L0_gnn_all = _L0_gnn_setup()
    _L0_gnn_in = {k: v for k, v in _L0_gnn_all.items() if k in ('W1', 'W2', 'W3', 'W4', 'W5', 'W6')}
    del _L0_gnn_all

    def _L1_gnn_setup():
        import jax, jax.numpy as jnp
        import numpy as np
        N = 4096
        IN_F = 256
        OUT_F = 256
        key = jax.random.key(seed)
        k1, k2, k3 = jax.random.split(key, 3)
        x = jax.random.normal(k1, (N, IN_F), dtype=jnp.float32)
        adj = jax.random.uniform(k2, (N, N), dtype=jnp.float32)
        W = jax.random.normal(k3, (IN_F, OUT_F), dtype=jnp.float32) * 0.1
        return {'x': x, 'adj': adj, 'W': W}
    _L1_gnn_all = _L1_gnn_setup()
    _L1_gnn_in = {k: v for k, v in _L1_gnn_all.items() if k in ('W',)}
    del _L1_gnn_all
    return {'x': x, 'adj': adj, 'L0_gnn_W1': _L0_gnn_in['W1'], 'L0_gnn_W2': _L0_gnn_in['W2'], 'L0_gnn_W3': _L0_gnn_in['W3'], 'L0_gnn_W4': _L0_gnn_in['W4'], 'L0_gnn_W5': _L0_gnn_in['W5'], 'L0_gnn_W6': _L0_gnn_in['W6'], 'L1_gnn_W': _L1_gnn_in['W']}

def reference(x, adj, L0_gnn_W1, L0_gnn_W2, L0_gnn_W3, L0_gnn_W4, L0_gnn_W5, L0_gnn_W6, L1_gnn_W):
    import jax
    import jax.numpy as jnp

    def _L0_gnn_ref(X, adj_, W1, W2, W3, W4, W5, W6):
        import jax, jax.numpy as jnp
        import numpy as np
        N = 4096
        INPUT_DIM = 256
        HIDDEN_DIM = 128

        def gcn_layer(adj, x, w):
            return jax.nn.relu(adj @ (x @ w))
        z = gcn_layer(adj_, X, W1)
        z = gcn_layer(adj_, z, W2)
        z = gcn_layer(adj_, z, W3)
        z = gcn_layer(adj_, z, W4)
        z = gcn_layer(adj_, z, W5)
        z = gcn_layer(adj_, z, W6)
        return z

    def _L1_gnn_ref(x, adj, W):
        import jax, jax.numpy as jnp
        import numpy as np
        N = 4096
        IN_F = 256
        OUT_F = 256
        n = adj.shape[0]
        adj_hat = adj + jnp.eye(n, dtype=adj.dtype)
        degree = adj_hat.sum(axis=1)
        d_inv_sqrt = degree ** (-0.5)
        adj_norm = d_inv_sqrt[:, None] * adj_hat * d_inv_sqrt[None, :]
        return jax.nn.relu(adj_norm @ x @ W)
    h = jnp.maximum(_layernorm(x, axis=-1), 0.0)
    x = x + _L0_gnn_ref(h, adj, L0_gnn_W1, L0_gnn_W2, L0_gnn_W3, L0_gnn_W4, L0_gnn_W5, L0_gnn_W6)
    h = jnp.maximum(_layernorm(x, axis=-1), 0.0)
    x = x + _L1_gnn_ref(h, adj, L1_gnn_W)
    return x

_drawn_inputs = setup_inputs


def setup_inputs(seed=0):
    import zlib

    import numpy as np

    out = dict(_drawn_inputs(seed))
    spreads = {}
    factors = {'L0_gnn_W1': 8.0,
     'L0_gnn_W2': 8.0,
     'L0_gnn_W3': 8.0,
     'L0_gnn_W4': 8.0,
     'L0_gnn_W5': 8.0,
     'L0_gnn_W6': 8.0}
    for name, (base, spread) in spreads.items():
        noise = np.random.default_rng([zlib.crc32(name.encode()), seed]).standard_normal(out[name].shape)
        drawn = base * np.exp(spread * noise) if base else spread * noise
        out[name] = jnp.asarray(drawn.astype(out[name].dtype))
    for name, factor in factors.items():
        out[name] = (out[name] * factor).astype(out[name].dtype)
    return out
```

```python
from contextlib import ExitStack

import concourse.bass as bass
from concourse import mybir

P = 128
F32 = mybir.dt.float32
F16 = mybir.dt.float16
I32 = mybir.dt.int32
ALU = mybir.AluOpType
ACT = mybir.ActivationFunctionType
AX = mybir.AxisListType
RMAX = bass.bass_isa.ReduceOp.max

EXPONENT = 0x7F800000
TINY = 1e-30
TO_HALF = 2.0 ** -14
EPS = 1e-5


def adjacency_net(nc, x, adj, w1, w2, w3, w4, w5, w6, w7, out):
    N, D = x.shape
    NC = N // P
    H = w1.shape[1]
    Q = w3.shape[1]
    IT = 512
    G = N // IT
    CG = IT // P
    LN_BOUND = float(D) ** 0.5
    assert D == 2 * P and H == P and 2 * Q == P and NC == G * CG

    x_v = x.rearrange("(c p) f -> p c f", p=P)
    out_v = out.rearrange("(c p) f -> p c f", p=P)

    with ExitStack() as ctx:
        def sb(name, shape, dt):
            return ctx.enter_context(nc.sbuf_tensor(name, shape, dt))

        def sem(name):
            return ctx.enter_context(nc.semaphore(name))

        at_hi = sb("at_hi", [P, NC, N], F16)
        at_lo = sb("at_lo", [P, NC, N], F16)
        ring = sb("ring", [P, CG, N], F32)
        xs = sb("xs", [P, NC, D], F32)
        z_hi = sb("z_hi", [P, 2, NC, P], F16)
        z_lo = sb("z_lo", [P, 2, NC, P], F16)
        wts = sb("wts", [P, 5 * P + Q], F32)
        w6s = sb("w6s", [P, D], F32)
        w7s = sb("w7s", [P, 2, D], F32)
        zT = sb("zT", [P, IT], F32)
        eye = sb("eye", [P, P], F32)
        eye16 = sb("eye16", [P, P], F16)
        eye2 = sb("eye2", [P, Q], F32)
        ones = sb("ones", [P, P], F32)
        stat = sb("stat", [P, CG, 6], F32)
        mv = sb("mv", [P, NC, 2], F32)
        var = sb("var", [P, NC], F32)
        half = sb("half", [P, NC], F32)
        rstd = sb("rstd", [P, NC], F32)
        nbias = sb("nbias", [P, NC], F32)
        rowsum = sb("rowsum", [P, NC], F32)
        rowmax = sb("rowmax", [P, NC], F32)
        t16 = sb("t16", [P, NC], F32)
        ainv = sb("ainv", [P, NC], F32)
        ascale = sb("ascale", [P, NC], F32)
        cnorm = sb("cnorm", [P, 8], F32)
        R = sb("R", [P, 1], F32)
        K = sb("K", [P, 8], F32)
        zmax = sb("zmax", [P, 8], F32)
        gmax = sb("gmax", [P, 8], F32)
        bnd = sb("bnd", [P, 8], F32)
        zinv = sb("zinv", [P, 8], F32)
        zmul = sb("zmul", [P, 8], F32)
        tab = sb("tab", [P, 8, NC], F32)
        dcol = sb("dcol", [P, NC], F32)
        dY = sb("dY", [P, NC], F32)
        dO = sb("dO", [P, NC], F32)
        sY = sb("sY", [P, 1], F32)

        W1 = wts[:, 0:2 * P].rearrange("p (h n) -> p h n", h=2)
        W2 = wts[:, 2 * P:3 * P]
        W3 = wts[:, 3 * P:3 * P + Q]
        W5 = wts[:, 3 * P + Q:4 * P + Q]
        W4 = wts[:, 4 * P + Q:5 * P + Q]
        h_ln = at_lo[:, :, N - IT:N].bitcast(F32)
        hT = at_hi[:, :, N - IT:N].bitcast(F32)
        absw = z_hi[:, 1, :, :].rearrange("p c f -> p (c f)").bitcast(F32)[:, 0:5 * P + Q]
        S = ring[:, 0, :]
        pT = ring[:, 1, 0:IT]
        tmp = ring[:, 1, IT:IT + CG * D].rearrange("p (c f) -> p c f", c=CG)
        y1 = ring[:, 2, :].bitcast(F16).rearrange("p (s c f) -> p s c f", s=2, c=NC)
        junk = z_lo[:, 1, :, :].rearrange("p c f -> p (c f)")

        acc = ctx.enter_context(nc.psum_tensor("acc", [P, G * IT], F32))
        work = ctx.enter_context(nc.psum_tensor("work", [P, G, IT], F32))
        work2 = work[:, 0:2, :].rearrange("p b n -> p (b n)").rearrange("p (c f) -> p c f", c=CG)
        last4 = [acc[:, 2 * IT:2 * IT + D], acc[:, 3 * IT:3 * IT + D], work[:, 2, 0:D], work[:, 3, 0:D]]

        x_in = [sem(f"x_in{g}") for g in range(G)]
        row_in = [sem(f"row_in{s}") for s in range(CG)]
        w_in = sem("w_in")
        w_late = sem("w_late")
        consts = sem("consts")
        eyes = sem("eyes")
        absw_done = sem("absw_done")
        norm_mm = sem("norm_mm")
        dve_step = sem("dve_step")
        pool_step = sem("pool_step")
        ln_var = sem("ln_var")
        ln_pow = sem("ln_pow")
        ln_ready = sem("ln_ready")
        h_done = sem("h_done")
        hT_mm = sem("hT_mm")
        hT_done = sem("hT_done")
        z_mm = sem("z_mm")
        z_act = sem("z_act")
        z_split = sem("z_split")
        abs_done = sem("abs_done")
        max_done = sem("max_done")
        a_scale = sem("a_scale")
        t_mm = sem("t_mm")
        a_hi = sem("a_hi")
        a_lo = sem("a_lo")
        acc_done = sem("acc_done")
        t_ready = sem("t_ready")
        z_scale = sem("z_scale")
        zmax_done = sem("zmax_done")
        gmax_done = sem("gmax_done")
        mid_mm = sem("mid_mm")
        mid_relu = sem("mid_relu")
        deg_dve = sem("deg_dve")
        deg_pool = sem("deg_pool")
        deg_mm = sem("deg_mm")
        deg_sum = sem("deg_sum")
        deg_pow = sem("deg_pow")
        x1_done = sem("x1_done")
        yt_mm = sem("yt_mm")
        gw_mm = sem("gw_mm")
        o_relu = sem("o_relu")
        o_done = sem("o_done")
        stored = sem("stored")

        WDMAS = 6
        WARM = (12, 6)
        block = ctx.enter_context(nc.Block())

        def hT_places(g):
            return (hT[:, CG * g:CG * g + CG, :],
                    acc[:, (g % 2) * 2 * IT:(g % 2 + 1) * 2 * IT].rearrange("p (c n) -> p c n", c=CG))

        @block.sync
        def _(sp):
            def load_x(g):
                sp.dma_start(xs[:, CG * g:CG * g + CG, :], x_v[:, CG * g:CG * g + CG, :]).then_inc(x_in[g], 16)

            load_x(0)
            load_x(1)
            for dst, src in ((W1, w1.rearrange("(h p) n -> p h n", p=P)), (W2, w2), (W3, w3), (W5, w5),
                             (W4[0:Q, :], w4), (W4[Q:P, :], w4)):
                sp.dma_start(dst, src).then_inc(w_in, 16)
            load_x(2)
            load_x(3)
            for s in range(CG):
                sp.dma_start(ring[:, s, :], adj[s * P:(s + 1) * P, :]).then_inc(row_in[s], 16)
            sp.dma_start(w6s[:, :], w6).then_inc(w_late, 16)
            sp.dma_start(w7s[:, :, :], w7.rearrange("(h p) n -> p h n", p=P)).then_inc(w_late, 16)
            for g in range(1, G):
                for s in range(CG):
                    sp.wait_ge(t_mm, g * 16 + (4 * s - 12))
                    sp.wait_ge(abs_done, g * 4 + (s - 3))
                    sp.dma_start(ring[:, s, :], adj[g * IT + s * P:g * IT + (s + 1) * P, :]).then_inc(row_in[s], 16)
            stores = [CG * g for g in range(G)] + [NC - 2, NC - 1, NC]
            for c, d in zip(stores, stores[1:]):
                sp.wait_ge(o_done, d)
                sp.dma_start(out_v[:, c:d, :], xs[:, c:d, :]).then_inc(stored, 16)
            sp.wait_ge(stored, 16 * (len(stores) - 1))

        @block.gpsimd
        def _(pool):
            nc.gpsimd.memset(half[:, :], -0.5).then_inc(consts, 1)
            nc.gpsimd.memset(ones[:, :], 1.0).then_inc(consts, 1)
            nc.gpsimd.memset(eye[:, :], 0.0).then_inc(pool_step, 1)
            pool.wait_ge(pool_step, 1)
            nc.gpsimd.affine_select(out=eye[:, :], in_=eye[:, :], compare_op=ALU.not_equal, fill=1.0, base=0,
                                    pattern=[[-1, P]], channel_multiplier=1).then_inc(consts, 1)
            pool.wait_ge(consts, 3)
            for g in range(G):
                pool.wait_ge(ln_var, g + 1)
                c = slice(CG * g, CG * g + CG)
                nc.gpsimd.tensor_tensor(rstd[:, c], var[:, c], half[:, c], ALU.pow).then_inc(ln_pow, 1)
                pool.wait_ge(ln_pow, g + 1)
                nc.gpsimd.tensor_tensor(nbias[:, c], t16[:, c], rstd[:, c], ALU.mult).then_inc(ln_ready, 1)
            for b in range(NC):
                pool.wait_ge(abs_done, b + 1)
                nc.gpsimd.partition_all_reduce(rowmax[:, b:b + 1], rowsum[:, b:b + 1], P,
                                               RMAX).then_inc(max_done, 1)
            pool.wait_ge(zmax_done, 1)
            nc.gpsimd.partition_all_reduce(gmax[:, 1:2], zmax[:, 1:2], P, RMAX).then_inc(gmax_done, 1)
            pool.wait_ge(a_lo, 4 * NC)
            nc.gpsimd.memset(S[:, 0:N // 2], 0.0).then_inc(deg_pool, 1)
            for l in range(4):
                pool.wait_ge(zmax_done, l + 2)
                nc.gpsimd.partition_all_reduce(gmax[:, l + 2:l + 3], zmax[:, l + 2:l + 3], P,
                                               RMAX).then_inc(gmax_done, 1)
                if l == 3:
                    break
                first, count = ((0, 8), (8, 4), (12, 4))[l]
                with pool.Fori(first, first + count) as c:
                    for n, part in enumerate((at_hi, at_lo)):
                        pool.wait_ge(deg_pool, c * 2 + (n + 1))
                        nc.gpsimd.tensor_tensor(S[:, 0:N // 2], S[:, 0:N // 2], part[:, c, 0:N // 2],
                                                ALU.add).then_inc(deg_pool, 1)
            pool.wait_ge(deg_sum, 1)
            nc.gpsimd.tensor_tensor(dcol[:, :], t16[:, :], half[:, :], ALU.pow).then_inc(deg_pow, 1)
            pool.wait_ge(zmax_done, 6)
            nc.gpsimd.partition_all_reduce(gmax[:, 7:8], zmax[:, 7:8], P, RMAX).then_inc(gmax_done, 1)
            with pool.Fori(0, G) as g:
                pool.wait_ge(ln_var, g + (G + 1))
                nc.gpsimd.tensor_tensor(rstd[:, bass.ds(g * CG, CG)], var[:, bass.ds(g * CG, CG)],
                                        half[:, 0:CG], ALU.pow).then_inc(ln_pow, 1)

        @block.scalar
        def _(act):
            act.wait_ge(w_in, 16 * WDMAS)
            nc.scalar.activation(absw, wts[:, :], ACT.Abs).then_inc(absw_done, 1)

            def hi_1(g):
                act.wait_ge(z_scale, 1)
                act.wait_ge(z_mm, g + 1)
                nc.scalar.activation(z_hi[:, 0, CG * g:CG * g + CG, :], work[:, g, :].rearrange(
                    "p (c f) -> p c f", c=CG), ACT.Copy, scale=zmul[:, 1:2]).then_inc(z_act, 1)

            def row_sums(b, s):
                nc.scalar.activation(junk, ring[:, s, :], ACT.Abs,
                                     accum_out=rowsum[:, bass.ds(b, 1)]).then_inc(abs_done, 1)


            def hT_copy(g):
                act.wait_ge(hT_mm, g + 1)
                nc.scalar.activation(*hT_places(g), ACT.Relu).then_inc(hT_done, 1)

            hT_copy(0)
            hi_1(0)
            hT_copy(1)
            hi_1(1)
            act.wait_ge(row_in[0], 16)
            row_sums(0, 0)
            hT_copy(2)
            hT_copy(3)
            hi_1(2)
            hi_1(3)
            act.wait_ge(row_in[1], 16)
            act.wait_ge(abs_done, 1)
            row_sums(1, 1)

            def adjacency_group(g, first=False, last=False):
                for s in range(CG):
                    t = (s + 1) % CG
                    if not (first and t == 1) and not (last and t == 0):
                        act.wait_ge(row_in[t], g * 16 + (16 if t else 32))
                        act.wait_ge(abs_done, g * CG + (s + 1))
                        row_sums(g * CG + (s + 1), t)
                    act.wait_ge(a_scale, g * CG + (s + 1))
                    for q in range(4):
                        act.wait_ge(t_mm, g * 16 + (4 * s + q + 1))
                        nc.scalar.activation(at_hi[:, 4 * q:4 * q + 4, bass.ds(g * IT + s * P, P)],
                                             work[:, q, :].rearrange("p (c f) -> p c f", c=4), ACT.Copy,
                                             scale=ascale[:, bass.ds(g * CG + s, 1)]).then_inc(a_hi, 1)

            adjacency_group(0, first=True)
            with act.Fori(1, G - 1) as g:
                adjacency_group(g)
            adjacency_group(G - 1, last=True)

            def z_bank(l, it, width):
                b = work[:, 0, :] if l == 5 else acc[:, bass.ds(it * IT, CG * width)]
                return b.rearrange("p (c f) -> p c f", c=CG)

            def hi(l, it, width, relu=False):
                act.wait_ge(z_mm, it + (4 * l + 1))
                if relu:
                    act.wait_ge(z_split, it + 4 * l)
                    nc.scalar.activation(tmp[:, :, 0:Q], z_bank(l, it, Q), ACT.Relu, scale=zmul[:, l + 1:l + 2]).then_inc(z_act, 1)
                else:
                    nc.scalar.activation(z_hi[:, l % 2, bass.ds(it * CG, CG), 0:width],
                                         z_bank(l, it, width), ACT.Copy,
                                         scale=zmul[:, l + 1:l + 2]).then_inc(z_act, 1)

            for l in range(1, 6):
                act.wait_ge(z_scale, l + 1)
                with act.Fori(0, G) as it:
                    if l == 4:
                        act.wait_ge(mid_mm, it + 1)
                        nc.scalar.activation(zT[:, :], work[:, it, :], ACT.Relu).then_inc(mid_relu, 1)
                    hi(l, it, Q if l == 2 else P, relu=l == 3)
            with act.Fori(0, G) as it:
                act.wait_ge(ln_ready, it + (G + 1))
                act.wait_ge(z_split, it + 4 * 6)
                for c in range(CG):
                    k = it * CG + c
                    last = nc.scalar.activation(tmp[:, c, :], xs[:, k, :], ACT.Relu, scale=rstd[:, bass.ds(k, 1)],
                                                bias=nbias[:, bass.ds(k, 1)])
                last.then_inc(z_act, 1)
            act.wait_ge(z_split, 4 * 7)

            def result_relu(it):
                act.wait_ge(gw_mm, it * CG + 1)
                for c in range(CG):
                    if c:
                        act.wait_ge(gw_mm, it * CG + (c + 1))
                    nc.scalar.activation(tmp[:, c, :], last4[c], ACT.Relu,
                                         scale=dO[:, bass.ds(it * CG + c, 1)]).then_inc(o_relu, 1)

            result_relu(0)
            with act.Fori(1, G) as it:
                act.wait_ge(o_done, it * CG)
                result_relu(it)

        @block.vector
        def _(dve):
            steps = [0]

            def step(ins):
                steps[0] += 1
                ins.then_inc(dve_step, 1)
                dve.wait_ge(dve_step, steps[0])

            def loop_step(ins, i, per, n):
                if per == 0:
                    step(ins)
                    return
                ins.then_inc(dve_step, 1)
                dve.wait_ge(dve_step, i * per + (steps[0] + n))

            def scale_of(l, bound, target=TO_HALF):
                step(nc.vector.tensor_scalar(bnd[:, l:l + 1], bound, TINY, target, ALU.max, ALU.mult))
                step(nc.vector.tensor_scalar(zinv[:, l:l + 1].bitcast(I32), bnd[:, l:l + 1].bitcast(I32), EXPONENT,
                                             None, ALU.bitwise_and))
                step(nc.vector.reciprocal(zmul[:, l:l + 1], zinv[:, l:l + 1]))

            dve.wait_ge(consts, 3)
            nc.vector.tensor_copy(eye16[:, :], eye[:, :]).then_inc(eyes, 1)
            nc.vector.tensor_tensor(eye2[:, :], eye[:, 0:Q], eye[:, Q:P], ALU.add).then_inc(eyes, 1)

            def ln_stats(g):
                dve.wait_ge(x_in[g], 16)
                for c in range(CG):
                    last = nc.vector.bn_stats(stat[:, c, :], xs[:, CG * g + c, :])
                step(last)
                for c in range(CG):
                    last = nc.vector.bn_aggr(mv[:, CG * g + c, :], stat[:, c, :])
                step(last)
                c = slice(CG * g, CG * g + CG)
                nc.vector.tensor_scalar(t16[:, c], mv[:, c, 0], -1.0, None, ALU.mult)
                nc.vector.tensor_scalar(var[:, c], mv[:, c, 1], EPS, None, ALU.add).then_inc(ln_var, 1)

            def ln_apply(g):
                dve.wait_ge(ln_ready, g + 1)
                for k in range(CG * g, CG * g + CG):
                    last = nc.vector.tensor_scalar(h_ln[:, k, :], xs[:, k, :], rstd[:, k:k + 1], nbias[:, k:k + 1],
                                                   ALU.mult, ALU.add)
                last.then_inc(h_done, 1)

            def lo_1(g):
                dve.wait_ge(z_act, g + 1)
                c = slice(CG * g, CG * g + CG)
                nc.vector.scalar_tensor_tensor(
                    out=z_lo[:, 0, c, :], in0=work[:, g, :].rearrange("p (c f) -> p c f", c=CG),
                    scalar=zmul[:, 1:2], in1=z_hi[:, 0, c, :], op0=ALU.mult,
                    op1=ALU.subtract).then_inc(z_split, 1)

            ln_stats(0)
            ln_stats(1)
            ln_apply(0)
            ln_stats(2)
            ln_apply(1)
            dve.wait_ge(norm_mm, 1)
            for l, src in ((1, work[:, 3, 0:P]), (2, work[:, 3, P:2 * P]), (3, work[:, 3, 2 * P:2 * P + Q]),
                           (5, work[:, 3, 2 * P + Q:3 * P + Q]), (4, work[:, 2, 0:P])):
                last = nc.vector.tensor_reduce(cnorm[:, l:l + 1], src, AX.X, ALU.max)
            step(last)
            step(nc.vector.tensor_scalar(bnd[:, 0:1], cnorm[:, 1:2], LN_BOUND, None, ALU.mult))
            scale_of(1, bnd[:, 0:1])
            nc.vector.tensor_copy(bnd[:, 7:8], bnd[:, 0:1]).then_inc(z_scale, 1)
            ln_stats(3)
            ln_apply(2)
            lo_1(0)
            ln_apply(3)
            lo_1(1)
            lo_1(2)
            lo_1(3)

            def z_maximum(l, width):
                nc.vector.tensor_reduce(zmax[:, l:l + 1], z_hi[:, (l - 1) % 2, :, 0:width], AX.XY, ALU.max,
                                        apply_absolute_value=True).then_inc(zmax_done, 1)

            def adjacency_block(b, i, per, between=None):
                n = bass.ds(b, 1)
                dve.wait_ge(max_done, b + 1)
                loop_step(nc.vector.tensor_scalar(t16[:, n], rowmax[:, n], TINY, TO_HALF, ALU.max, ALU.mult), i, per, 1)
                loop_step(nc.vector.tensor_scalar(ainv[:, n].bitcast(I32), t16[:, n].bitcast(I32), EXPONENT, None,
                                                  ALU.bitwise_and), i, per, 2)
                nc.vector.reciprocal(ascale[:, n], ainv[:, n]).then_inc(a_scale, 1)
                if between:
                    between()
                for q in range(4):
                    dve.wait_ge(a_hi, b * 4 + (q + 1))
                    at = bass.ds(b * P, P)
                    nc.vector.scalar_tensor_tensor(
                        out=at_lo[:, 4 * q:4 * q + 4, at], in0=work[:, q, :].rearrange("p (c f) -> p c f", c=4),
                        scalar=ascale[:, n], in1=at_hi[:, 4 * q:4 * q + 4, at], op0=ALU.mult,
                        op1=ALU.subtract).then_inc(a_lo, 1)

            def off_scales(dst, it, table, relu=False):
                t = table.unsqueeze(2).to_broadcast([P, CG, P])
                src = acc[:, bass.ds(it * IT, IT)].rearrange("p (c n) -> p c n", c=CG)
                d = dst[:, :].rearrange("p (c n) -> p c n", c=CG)
                if relu:
                    return nc.vector.scalar_tensor_tensor(out=d, in0=src, scalar=0.0, in1=t, op0=ALU.max,
                                                          op1=ALU.mult)
                return nc.vector.tensor_tensor(d, src, t, ALU.mult)

            def evacuate(l, it, relu):
                dve.wait_ge(acc_done, it + (4 * (l - 1) + 1))
                table = ainv[:, bass.ds(it * CG, CG)] if l == 1 else tab[:, l, bass.ds(it * CG, CG)]
                off_scales(pT if l in (4, 6) else zT, it, table, relu).then_inc(t_ready, 1)

            def lo(l, it, width):
                dve.wait_ge(z_act, it + (4 * l + 1))
                c = bass.ds(it * CG, CG)
                if width == P:
                    dst = z_lo[:, l % 2, c, :]
                else:
                    dst = z_hi[:, l % 2, c, Q:P]
                src = work[:, 0, :] if l == 5 else acc[:, bass.ds(it * IT, CG * width)]
                nc.vector.scalar_tensor_tensor(
                    out=dst, in0=src.rearrange("p (c f) -> p c f", c=CG),
                    scalar=zmul[:, l + 1:l + 2], in1=z_hi[:, l % 2, c, 0:width], op0=ALU.mult,
                    op1=ALU.subtract).then_inc(z_split, 1)

            def next_scale(l):
                dve.wait_ge(gmax_done, l)
                step(nc.vector.tensor_scalar(bnd[:, l:l + 1], gmax[:, l:l + 1], zinv[:, l:l + 1], K[:, l + 1:l + 2],
                                             ALU.mult, ALU.mult))
                scale_of(l + 1, bnd[:, l:l + 1])
                if l == 1:
                    step(nc.vector.tensor_tensor(zmul[:, 2:3], zmul[:, 2:3], zinv[:, 1:2], ALU.mult))
                step(nc.vector.tensor_scalar(tab[:, l + 1, :], ainv[:, :], zinv[:, l + 1:l + 2], None, ALU.mult))
                nc.vector.tensor_copy(bnd[:, 7:8], bnd[:, 0:1]).then_inc(z_scale, 1)

            def sum_chunk(j, done):
                for n, part in enumerate((at_hi, at_lo)):
                    dve.wait_ge(deg_dve, done + n)
                    nc.vector.tensor_tensor(S[:, N // 2:N], S[:, N // 2:N], part[:, j, N // 2:N],
                                            ALU.add).then_inc(deg_dve, 1)

            def bounds():
                dve.wait_ge(max_done, NC)
                step(nc.vector.tensor_reduce(R[:, :], rowmax[:, :], AX.X, ALU.max))
                nc.vector.tensor_scalar(K[:, 2:4], cnorm[:, 2:4], R[:, 0:1], None, ALU.mult)
                nc.vector.tensor_copy(K[:, 4:5], R[:, :])
                nc.vector.tensor_copy(K[:, 6:7], R[:, :])
                step(nc.vector.tensor_scalar(K[:, 5:6], cnorm[:, 5:6], R[:, 0:1], cnorm[:, 4:5], ALU.mult, ALU.mult))
                next_scale(1)

            with dve.Fori(0, CG) as b:
                adjacency_block(b, b, 2)
            steps[0] += 2 * CG
            dve.wait_ge(z_split, 4)
            z_maximum(1, P)
            with dve.Fori(1, G - 1) as g:
                for s in range(CG):
                    adjacency_block(g * CG + s, (g - 1) * CG + s, 2)
                    if s == 1:
                        evacuate(1, g - 1, True)
            steps[0] += 2 * CG * (G - 2)
            for s in range(CG):
                adjacency_block((G - 1) * CG + s, 0, 0, bounds if s == CG - 1 else None)
                if s == 1:
                    evacuate(1, G - 2, True)
            with dve.Fori(0, G - 1) as it:
                lo(1, it, P)
            evacuate(1, G - 1, True)
            lo(1, G - 1, P)
            dve.wait_ge(z_split, 4 * 2)

            def split(l, it):
                if l == 3:
                    dve.wait_ge(z_act, it + (4 * l + 1))
                    c = bass.ds(it * CG, CG)
                    loop_step(nc.vector.tensor_copy(z_hi[:, 1, c, 0:Q], tmp[:, :, 0:Q]), it, 1, 1)
                    nc.vector.tensor_tensor(z_hi[:, 1, c, Q:P], tmp[:, :, 0:Q], z_hi[:, 1, c, 0:Q],
                                            ALU.subtract).then_inc(z_split, 1)
                else:
                    lo(l, it, Q if l == 2 else P)

            def degrees():
                dve.wait_ge(deg_mm, 1)
                step(nc.vector.tensor_tensor(t16[:, :], work[:, 3, 0:NC], ainv[:, :], ALU.mult))
                nc.vector.tensor_scalar(t16[:, :], t16[:, :], 1.0, None, ALU.add).then_inc(deg_sum, 1)

            def degree_scale():
                dve.wait_ge(deg_pow, 1)
                nc.vector.tensor_reduce(zmax[:, 7:8], dcol[:, :], AX.X, ALU.max).then_inc(zmax_done, 1)
                dve.wait_ge(gmax_done, 6)
                step(nc.vector.tensor_scalar(bnd[:, 6:7], gmax[:, 7:8], LN_BOUND, None, ALU.mult))
                scale_of(7, bnd[:, 6:7])
                nc.vector.tensor_scalar(dY[:, :], dcol[:, :], zmul[:, 7:8], None, ALU.mult)
                step(nc.vector.tensor_scalar(dO[:, :], dcol[:, :], zinv[:, 7:8], None, ALU.mult))

            for l, first, count in ((2, 1, 3), (3, 10, 1), (4, 13, 1)):
                z_maximum(l, Q if l in (3, 4) else P)
                next_scale(l)
                if l == 2:
                    nc.vector.tensor_tensor(S[:, N // 2:N], at_hi[:, 0, N // 2:N], at_lo[:, 0, N // 2:N],
                                            ALU.add).then_inc(deg_dve, 1)
                with dve.Fori(0, G - 1) as it:
                    evacuate(l, it, relu=l == 2)
                    split(l, it)
                    for k in range(count):
                        sum_chunk(it * count + (first + k), it * (2 * count) + (2 * (first + k) - 1))
                evacuate(l, G - 1, relu=l == 2)
                split(l, G - 1)
                if l == 3:
                    steps[0] += G
                dve.wait_ge(z_split, 4 * (l + 1))
            z_maximum(5, P)
            next_scale(5)
            for it in range(G):
                evacuate(5, it, relu=True)
                split(5, it)
                if it == 0:
                    degrees()
                if it == 1:
                    degree_scale()

            for it in range(G):
                evacuate(6, it, False)
                dve.wait_ge(z_mm, it + (4 * 6 + 1))
                c = slice(it * CG, it * CG + CG)
                nc.vector.scalar_tensor_tensor(out=xs[:, c, :], in0=work2, scalar=0.0, in1=xs[:, c, :], op0=ALU.max,
                                               op1=ALU.add).then_inc(x1_done, 1)
                dve.wait_ge(x1_done, it + 1)
                for k in range(CG):
                    last = nc.vector.bn_stats(stat[:, k, :], xs[:, it * CG + k, :])
                step(last)
                for k in range(CG):
                    last = nc.vector.bn_aggr(mv[:, it * CG + k, :], stat[:, k, :])
                step(last)
                nc.vector.tensor_scalar(var[:, c], mv[:, c, 1], EPS, None, ALU.add).then_inc(ln_var, 1)
                dve.wait_ge(ln_pow, it + (G + 1))
                step(nc.vector.tensor_tensor(rstd[:, c], rstd[:, c], dY[:, c], ALU.mult))
                nc.vector.scalar_tensor_tensor(out=nbias[:, c], in0=mv[:, c, 0], scalar=-1.0, in1=rstd[:, c],
                                               op0=ALU.mult, op1=ALU.mult).then_inc(ln_ready, 1)
                dve.wait_ge(z_act, it + (4 * 6 + 1))
                nc.vector.tensor_copy(z_hi[:, 0, c, :], tmp[:, :, 0:P])
                step(nc.vector.tensor_copy(y1[:, 0, c, :], tmp[:, :, P:D]))
                nc.vector.tensor_tensor(z_lo[:, 0, c, :], tmp[:, :, 0:P], z_hi[:, 0, c, :], ALU.subtract)
                nc.vector.tensor_tensor(y1[:, 1, c, :], tmp[:, :, P:D], y1[:, 0, c, :],
                                        ALU.subtract).then_inc(z_split, 1)

            with dve.Fori(0, G) as it:
                for h, dst in enumerate((pT, zT)):
                    dve.wait_ge(acc_done, it * 2 + (4 * 6 + h + 1))
                    t = ainv[:, bass.ds(it * CG, CG)].unsqueeze(2).to_broadcast([P, CG, P])
                    loop_step(nc.vector.tensor_tensor(
                        dst[:, :].rearrange("p (c n) -> p c n", c=CG),
                        acc[:, h * IT:(h + 1) * IT].rearrange("p (c n) -> p c n", c=CG), t, ALU.mult), it, 2, h + 1)
                    dve.wait_ge(yt_mm, it + 1)
                    nc.vector.tensor_tensor(dst[:, :], dst[:, :], work[:, h, :], ALU.add).then_inc(t_ready, 1)
                for c in range(CG):
                    dve.wait_ge(o_relu, it * CG + (c + 1))
                    k = it * CG + c
                    nc.vector.tensor_tensor(xs[:, k, :], xs[:, k, :], tmp[:, c, :], ALU.add).then_inc(o_done, 1)

        @block.tensor
        def _(pe):
            def keep_warm(n):
                for _ in range(n):
                    nc.tensor.matmul(work[:, 0, 0:P], ones[:, :], ones[:, :], start=True, stop=True)

            pe.wait_ge(consts, 3)
            keep_warm(WARM[0])
            pe.wait_ge(absw_done, 1)
            nc.tensor.matmul(work[:, 3, 0:P], ones[:, :], absw[:, 0:P], start=True, stop=False)
            nc.tensor.matmul(work[:, 3, 0:P], ones[:, :], absw[:, P:2 * P], start=False, stop=True)
            nc.tensor.matmul(work[:, 3, P:3 * P + Q], ones[:, :], absw[:, 2 * P:4 * P + Q], start=True, stop=True)
            nc.tensor.matmul(work[:, 2, 0:P], ones[0:Q, :], absw[0:Q, 4 * P + Q:5 * P + Q], start=True,
                             stop=True).then_inc(norm_mm, 1)

            def ln_transposes(g):
                pe.wait_ge(h_done, g + 1)
                if g >= 2:
                    pe.wait_ge(hT_done, g - 1)
                for c in range(CG):
                    for h in range(2):
                        n = (g % 2) * 2 * IT + (2 * c + h) * P
                        last = nc.tensor.transpose(acc[:, n:n + P], h_ln[:, CG * g + c, h * P:(h + 1) * P], eye[:, :])
                last.then_inc(hT_mm, 1)

            def first_z(g):
                pe.wait_ge(hT_done, g + 1)
                if g >= 2:
                    pe.wait_ge(z_scale, 1)
                for c in range(CG):
                    for h in range(2):
                        last = nc.tensor.matmul(work[:, g, c * P:(c + 1) * P], hT[:, CG * g + c, h * P:(h + 1) * P], W1[:, h, :],
                                                start=h == 0, stop=h == 1)
                last.then_inc(z_mm, 1)

            keep_warm(WARM[1])
            ln_transposes(0)
            ln_transposes(1)
            first_z(0)
            ln_transposes(2)
            first_z(1)
            ln_transposes(3)
            first_z(2)
            first_z(3)

            def transposes(g, s, q):
                if q == 0:
                    pe.wait_ge(row_in[s], g * 16 + 16)
                for k in range(4):
                    n = (4 * q + k) * P
                    last = nc.tensor.transpose(work[:, q, k * P:(k + 1) * P], ring[:, s, n:n + P], eye[:, :])
                last.then_inc(t_mm, 1)

            for s in range(2):
                for q in range(4):
                    if s == 0:
                        pe.wait_ge(z_split, q + 1)
                    else:
                        pe.wait_ge(a_lo, 4 * (s - 1) + q + 1)
                    transposes(0, s, q)

            def products(l, out_, j, i, first=False, last=False, n=IT):
                if l == 7:
                    zh, zl = z_hi[:, 0, j, :], z_lo[:, 0, j, :]
                elif l == 8:
                    zh, zl = y1[:, 0, j, :], y1[:, 1, j, :]
                else:
                    zh, zl = z_hi[:, (l - 1) % 2, j, :], z_lo[:, (l - 1) % 2, j, :]
                a, b = at_hi[:, j, bass.ds(i, n)], at_lo[:, j, bass.ds(i, n)]
                nc.tensor.matmul(out_, zh, b, start=first, stop=False)
                if l in (3, 4):
                    return nc.tensor.matmul(out_, zh, a, start=False, stop=last)
                nc.tensor.matmul(out_, zl, a, start=False, stop=False)
                return nc.tensor.matmul(out_, zh, a, start=False, stop=last)

            def unit(l, out_, i, slot_a=None, slot_b=None, before_last=None, js=range(NC)):
                between = {2: slot_a, 7: slot_b, 12: before_last}
                for j in js:
                    if between.get(j):
                        between[j]()
                    done = products(l, out_, j, i, first=j == 0, last=j == NC - 1)
                if js[-1] == NC - 1:
                    done.then_inc(acc_done, 1)

            def bank(it):
                return acc[:, bass.ds(it * IT, IT)]

            def to_nodes(l, it, w, width):
                pe.wait_ge(t_ready, it + (4 * (l - 1) + 1))
                for c in range(CG):
                    last = nc.tensor.matmul(acc[:, bass.ds(it * IT + c * width, width)], zT[:, c * P:(c + 1) * P], w,
                                            start=True, stop=True)
                last.then_inc(z_mm, 1)

            def small_a(l, it):
                if l == 1:
                    to_nodes(1, it, W2, H)
                elif l == 2:
                    to_nodes(2, it, W3, Q)
                elif l == 3:
                    to_nodes(3, it, eye2[:, :], Q)
                elif l == 4:
                    pe.wait_ge(t_ready, it + (4 * 3 + 1))
                    nc.tensor.matmul(work[:, it, :], W4, pT[:, :], start=True, stop=True).then_inc(mid_mm, 1)
                elif l == 5:
                    pe.wait_ge(t_ready, it + (4 * 4 + 1))
                    pe.wait_ge(z_split, it + 4 * 5)
                    for c in range(CG):
                        last = nc.tensor.transpose(work[:, 0, c * P:(c + 1) * P], zT[:, c * P:(c + 1) * P], eye[:, :])
                    last.then_inc(z_mm, 1)
                elif l == 6:
                    pe.wait_ge(t_ready, it + (4 * 5 + 1))
                    for c in range(CG):
                        last = nc.tensor.matmul(work2[:, c, :], pT[:, c * P:(c + 1) * P], w6s[:, :], start=True,
                                                stop=True)
                    last.then_inc(z_mm, 1)

            def small_b(l, it):
                if l == 4:
                    pe.wait_ge(mid_relu, it + 1)
                    for c in range(CG):
                        last = nc.tensor.matmul(acc[:, bass.ds(it * IT + c * P, P)], zT[:, c * P:(c + 1) * P], W5,
                                                start=True, stop=True)
                    last.then_inc(z_mm, 1)

            def first_layer_unit(g, small=True, last=False):
                for h in range(2):
                    for j in range(NC):
                        if j % 4 == 0:
                            pe.wait_ge(a_lo, g * 16 + (8 * h + 5 + j // 4))
                        done = products(1, acc[:, bass.ds(g * IT + h * IT // 2, IT // 2)], j, g * IT + h * IT // 2,
                                        first=j == 0, last=j == NC - 1, n=IT // 2)
                        if j % 2 == 1 and not (last and h == 1):
                            k = 8 * (h + 1) + j // 2
                            pe.wait_ge(a_lo, g * 16 + (k - 3))
                            transposes(g + k // 16, k // 4 % CG, k % 4)
                        if small and h == 1 and j == 2:
                            small_a(1, g - 1)
                done.then_inc(acc_done, 1)

            pe.wait_ge(z_split, 4)
            first_layer_unit(0, small=False)
            with pe.Fori(1, G - 1) as g:
                first_layer_unit(g)
            first_layer_unit(G - 1, last=True)

            def degree_sums():
                pe.wait_ge(deg_dve, 2 * NC - 1)
                pe.wait_ge(deg_pool, 2 * NC + 1)
                for c in range(NC):
                    last = nc.tensor.matmul(work[:, 3, c:c + 1], S[:, c * P:(c + 1) * P], ones[:, 0:1], start=True,
                                            stop=True)
                last.then_inc(deg_mm, 1)

            def slots(l, it):
                return {"slot_a": lambda: small_a(l, it), "slot_b": lambda: small_b(l, it)}

            for l in range(2, 7):
                pe.wait_ge(z_split, 4 * (l - 1) + 3)
                unit(l, bank(0), 0, **slots(l - 1, G - 1), before_last=lambda: pe.wait_ge(z_split, 4 * l))
                if l == 5:
                    degree_sums()
                if l < 6:
                    with pe.Fori(1, G) as it:
                        unit(l, bank(it), it * IT, **slots(l, it - 1))
            pe.wait_ge(w_late, 32)
            unit(6, bank(1), IT, **slots(6, 0))
            with pe.Fori(2, G) as it:
                pe.wait_ge(x1_done, it - 1)
                unit(6, bank(it), it * IT, **slots(6, it - 1))

            def y_transposed(it):
                for h in range(2):
                    for c in range(CG):
                        j = it * CG + c
                        zh, zl = (z_hi[:, 0, j, :], z_lo[:, 0, j, :]) if h == 0 else (y1[:, 0, j, :], y1[:, 1, j, :])
                        o = work[:, h, c * P:(c + 1) * P]
                        nc.tensor.matmul(o, zl, eye16[:, :], start=True, stop=False)
                        last = nc.tensor.matmul(o, zh, eye16[:, :], start=False, stop=True)
                last.then_inc(yt_mm, 1)

            def last_product(it, h):
                pe.wait_ge(t_ready, it * 2 + (4 * 6 + 1 + h))
                if h == 0:
                    with_previous = it * CG
                    if not (type(it) is int and it == 0):
                        pe.wait_ge(o_relu, with_previous)
                for c in range(CG):
                    done = nc.tensor.matmul(last4[c], (pT, zT)[h][:, c * P:(c + 1) * P], w7s[:, h, :], start=h == 0,
                                            stop=h == 1)
                    if h == 1:
                        done.then_inc(gw_mm, 1)

            def last_small():
                pe.wait_ge(x1_done, G - 1)
                small_a(6, G - 1)

            pe.wait_ge(eyes, 2)
            pe.wait_ge(z_split, 4 * 6 + 3)
            early, late = range(12), range(12, NC)
            unit(7, bank(0), 0, slot_a=last_small, js=early)
            unit(8, bank(1), 0, js=early)
            pe.wait_ge(x1_done, G)
            y_transposed(0)
            pe.wait_ge(z_split, 4 * 7)
            unit(7, bank(0), 0, js=late)
            unit(8, bank(1), 0, js=late)
            pe.wait_ge(w_late, 32)
            pe.wait_ge(t_ready, 4 * 6 + 1)
            last_product(0, 0)
            with pe.Fori(1, G) as it:
                unit(7, bank(0), it * IT, slot_a=lambda: last_product(it - 1, 1))
                unit(8, bank(1), it * IT, slot_a=lambda: y_transposed(it), slot_b=lambda: last_product(it, 0))
            last_product(G - 1, 1)


_INS = ["x", "adj", "L0_gnn_W1", "L0_gnn_W2", "L0_gnn_W3", "L0_gnn_W4", "L0_gnn_W5", "L0_gnn_W6", "L1_gnn_W"]


def kernel(**inputs):
    import numpy as _np
    import concourse.bacc as _bacc
    from concourse import mybir as _mybir
    from concourse.bass_utils import run_bass_kernel_spmd as _run

    nc = _bacc.Bacc("TRN2", target_bir_lowering=False, num_devices=1)
    arrays, args = {}, []
    for name in _INS:
        a = _np.ascontiguousarray(inputs[name])
        arrays[f"in_{name}"] = a
        args.append(nc.dram_tensor(f"in_{name}", a.shape, _mybir.dt.from_np(a.dtype), kind="ExternalInput").ap())
    out = nc.dram_tensor("out", arrays["in_x"].shape, _mybir.dt.float32, kind="ExternalOutput").ap()
    adjacency_net(nc, *args, out)
    return _run(nc, [arrays], core_ids=[0]).results[0]["out"]
```

```python
from contextlib import ExitStack

import concourse.bass as bass
from concourse import mybir

P = 128
F32 = mybir.dt.float32
F16 = mybir.dt.float16
I32 = mybir.dt.int32
ALU = mybir.AluOpType
ACT = mybir.ActivationFunctionType
AX = mybir.AxisListType
RMAX = bass.bass_isa.ReduceOp.max

EXPONENT = 0x7F800000
TINY = 1e-30
TO_HALF = 2.0 ** -14
EPS = 1e-5


def adjacency_net(nc, x, adj, w1, w2, w3, w4, w5, w6, w7, out):
    N, D = x.shape
    NC = N // P
    H = w1.shape[1]
    Q = w3.shape[1]
    IT = 512
    G = N // IT
    CG = IT // P
    LN_BOUND = float(D) ** 0.5
    assert D == 2 * P and H == P and 2 * Q == P and NC == G * CG

    x_v = x.rearrange("(c p) f -> p c f", p=P)
    out_v = out.rearrange("(c p) f -> p c f", p=P)

    with ExitStack() as ctx:
        def sb(name, shape, dt):
            return ctx.enter_context(nc.sbuf_tensor(name, shape, dt))

        def sem(name):
            return ctx.enter_context(nc.semaphore(name))

        at_hi = sb("at_hi", [P, NC, N], F16)
        at_lo = sb("at_lo", [P, NC, N], F16)
        ring = sb("ring", [P, CG, N], F32)
        xs = sb("xs", [P, NC, D], F32)
        z_hi = sb("z_hi", [P, 2, NC, P], F16)
        z_lo = sb("z_lo", [P, 2, NC, P], F16)
        wts = sb("wts", [P, 5 * P + Q], F32)
        w6s = sb("w6s", [P, D], F32)
        w7s = sb("w7s", [P, 2, D], F32)
        zT = sb("zT", [P, IT], F32)
        eye = sb("eye", [P, P], F32)
        eye16 = sb("eye16", [P, P], F16)
        eye2 = sb("eye2", [P, Q], F32)
        ones = sb("ones", [P, P], F32)
        ones16 = sb("ones16", [P, 1], F16)
        stat = sb("stat", [P, CG, 6], F32)
        mv = sb("mv", [P, NC, 2], F32)
        var = sb("var", [P, NC], F32)
        half = sb("half", [P, NC], F32)
        rstd = sb("rstd", [P, NC], F32)
        nbias = sb("nbias", [P, NC], F32)
        rowsum = sb("rowsum", [P, NC], F32)
        rowmax = sb("rowmax", [P, NC], F32)
        t16 = sb("t16", [P, NC], F32)
        ainv = sb("ainv", [P, NC], F32)
        ascale = sb("ascale", [P, NC], F32)
        cnorm = sb("cnorm", [P, 8], F32)
        R = sb("R", [P, 1], F32)
        K = sb("K", [P, 8], F32)
        zmax = sb("zmax", [P, 8], F32)
        gmax = sb("gmax", [P, 8], F32)
        bnd = sb("bnd", [P, 8], F32)
        zinv = sb("zinv", [P, 8], F32)
        zmul = sb("zmul", [P, 8], F32)
        tab = sb("tab", [P, 8, NC], F32)
        dcol = sb("dcol", [P, NC], F32)
        dY = sb("dY", [P, NC], F32)
        dO = sb("dO", [P, NC], F32)
        sY = sb("sY", [P, 1], F32)

        W1 = wts[:, 0:2 * P].rearrange("p (h n) -> p h n", h=2)
        W2 = wts[:, 2 * P:3 * P]
        W3 = wts[:, 3 * P:3 * P + Q]
        W5 = wts[:, 3 * P + Q:4 * P + Q]
        W4 = wts[:, 4 * P + Q:5 * P + Q]
        h_ln = at_lo[:, :, N - IT:N].bitcast(F32)
        hT = at_hi[:, :, N - IT:N].bitcast(F32)
        absw = z_hi[:, 1, :, :].rearrange("p c f -> p (c f)").bitcast(F32)[:, 0:5 * P + Q]
        S = ring[:, 0, :]
        S16 = ring[:, 3, :].bitcast(F16).rearrange("p (s n) -> p s n", s=2)
        pT = ring[:, 1, 0:IT]
        tmp = ring[:, 1, IT:IT + CG * D].rearrange("p (c f) -> p c f", c=CG)
        y1 = ring[:, 2, :].bitcast(F16).rearrange("p (s c f) -> p s c f", s=2, c=NC)
        junk = z_lo[:, 1, :, :].rearrange("p c f -> p (c f)")

        acc = ctx.enter_context(nc.psum_tensor("acc", [P, G * IT], F32))
        work = ctx.enter_context(nc.psum_tensor("work", [P, G, IT], F32))
        work2 = work[:, 0:2, :].rearrange("p b n -> p (b n)").rearrange("p (c f) -> p c f", c=CG)
        last4 = [acc[:, 2 * IT:2 * IT + D], acc[:, 3 * IT:3 * IT + D], work[:, 2, 0:D], work[:, 3, 0:D]]

        x_in = [sem(f"x_in{g}") for g in range(G)]
        row_in = [sem(f"row_in{s}") for s in range(CG)]
        w_in = sem("w_in")
        w_late = sem("w_late")
        consts = sem("consts")
        eyes = sem("eyes")
        absw_done = sem("absw_done")
        norm_mm = sem("norm_mm")
        norm_read = sem("norm_read")
        dve_step = sem("dve_step")
        pool_step = sem("pool_step")
        ln_var = sem("ln_var")
        ln_pow = sem("ln_pow")
        ln_ready = sem("ln_ready")
        h_first = sem("h_first")
        h_done = sem("h_done")
        hT_mm = sem("hT_mm")
        hT_done = sem("hT_done")
        z_mm = sem("z_mm")
        z_act = sem("z_act")
        z_split = sem("z_split")
        abs_done = sem("abs_done")
        max_done = sem("max_done")
        a_scale = sem("a_scale")
        t_mm = sem("t_mm")
        a_hi = sem("a_hi")
        a_lo = sem("a_lo")
        acc_done = sem("acc_done")
        t_ready = sem("t_ready")
        z_scale = sem("z_scale")
        zmax1 = sem("zmax1")
        zmax_done = sem("zmax_done")
        gmax_done = sem("gmax_done")
        mid_mm = sem("mid_mm")
        mid_relu = sem("mid_relu")
        deg_dve = sem("deg_dve")
        deg_pool = sem("deg_pool")
        deg_split = sem("deg_split")
        deg_mm = sem("deg_mm")
        deg_sum = sem("deg_sum")
        deg_pow = sem("deg_pow")
        x1_done = sem("x1_done")
        yt_mm = sem("yt_mm")
        gw_mm = sem("gw_mm")
        o_relu = sem("o_relu")
        o_done = sem("o_done")
        stored = sem("stored")

        WDMAS = 6
        WARM = (12, 5, 2)
        block = ctx.enter_context(nc.Block())

        def hT_places(g):
            return (hT[:, CG * g:CG * g + CG, :],
                    acc[:, (g % 2) * 2 * IT:(g % 2 + 1) * 2 * IT].rearrange("p (c n) -> p c n", c=CG))

        @block.sync
        def _(sp):
            def load_x(g):
                sp.dma_start(xs[:, CG * g:CG * g + CG, :], x_v[:, CG * g:CG * g + CG, :]).then_inc(x_in[g], 16)

            load_x(0)
            load_x(1)
            for dst, src in ((W1, w1.rearrange("(h p) n -> p h n", p=P)), (W2, w2), (W3, w3), (W5, w5),
                             (W4[0:Q, :], w4), (W4[Q:P, :], w4)):
                sp.dma_start(dst, src).then_inc(w_in, 16)
            load_x(2)
            load_x(3)
            for s in range(CG):
                sp.dma_start(ring[:, s, :], adj[s * P:(s + 1) * P, :]).then_inc(row_in[s], 16)
            sp.dma_start(w6s[:, :], w6).then_inc(w_late, 16)
            sp.dma_start(w7s[:, :, :], w7.rearrange("(h p) n -> p h n", p=P)).then_inc(w_late, 16)
            for g in range(1, G):
                for s in range(CG):
                    sp.wait_ge(t_mm, g * 16 + (4 * s - 12))
                    sp.wait_ge(abs_done, g * 4 + (s - 3))
                    sp.dma_start(ring[:, s, :], adj[g * IT + s * P:g * IT + (s + 1) * P, :]).then_inc(row_in[s], 16)
            stores = [CG * g for g in range(G)] + [NC - 2, NC - 1, NC]
            for c, d in zip(stores, stores[1:]):
                sp.wait_ge(o_done, d)
                sp.dma_start(out_v[:, c:d, :], xs[:, c:d, :]).then_inc(stored, 16)
            sp.wait_ge(stored, 16 * (len(stores) - 1))

        @block.gpsimd
        def _(pool):
            nc.gpsimd.memset(half[:, :], -0.5).then_inc(consts, 1)
            nc.gpsimd.memset(ones[:, :], 1.0).then_inc(consts, 1)
            nc.gpsimd.memset(eye[:, :], 0.0).then_inc(pool_step, 1)
            pool.wait_ge(pool_step, 1)
            nc.gpsimd.affine_select(out=eye[:, :], in_=eye[:, :], compare_op=ALU.not_equal, fill=1.0, base=0,
                                    pattern=[[-1, P]], channel_multiplier=1).then_inc(consts, 1)
            pool.wait_ge(consts, 3)
            for g in range(G):
                pool.wait_ge(ln_var, g + 1)
                c = slice(CG * g, CG * g + CG)
                nc.gpsimd.tensor_tensor(rstd[:, c], var[:, c], half[:, c], ALU.pow).then_inc(ln_pow, 1)
                pool.wait_ge(ln_pow, g + 1)
                nc.gpsimd.tensor_tensor(nbias[:, c], t16[:, c], rstd[:, c], ALU.mult).then_inc(ln_ready, 1)
            for b in range(NC):
                pool.wait_ge(abs_done, b + 1)
                nc.gpsimd.partition_all_reduce(rowmax[:, b:b + 1], rowsum[:, b:b + 1], P,
                                               RMAX).then_inc(max_done, 1)
            pool.wait_ge(zmax_done, 1)
            nc.gpsimd.partition_all_reduce(gmax[:, 1:2], zmax[:, 1:2], P, RMAX).then_inc(gmax_done, 1)
            pool.wait_ge(a_lo, 4 * NC)
            nc.gpsimd.memset(S[:, 0:N // 2], 0.0).then_inc(deg_pool, 1)
            for l in range(4):
                pool.wait_ge(zmax_done, l + 2)
                nc.gpsimd.partition_all_reduce(gmax[:, l + 2:l + 3], zmax[:, l + 2:l + 3], P,
                                               RMAX).then_inc(gmax_done, 1)
                if l == 3:
                    break
                first, count = ((0, 8), (8, 4), (12, 4))[l]
                with pool.Fori(first, first + count) as c:
                    for n, part in enumerate((at_hi, at_lo)):
                        pool.wait_ge(deg_pool, c * 2 + (n + 1))
                        nc.gpsimd.tensor_tensor(S[:, 0:N // 2], S[:, 0:N // 2], part[:, c, 0:N // 2],
                                                ALU.add).then_inc(deg_pool, 1)
            pool.wait_ge(deg_sum, 1)
            nc.gpsimd.tensor_tensor(dcol[:, :], t16[:, :], half[:, :], ALU.pow).then_inc(deg_pow, 1)
            pool.wait_ge(zmax_done, 6)
            nc.gpsimd.partition_all_reduce(gmax[:, 7:8], zmax[:, 7:8], P, RMAX).then_inc(gmax_done, 1)
            with pool.Fori(0, G) as g:
                pool.wait_ge(ln_var, g + (G + 1))
                nc.gpsimd.tensor_tensor(rstd[:, bass.ds(g * CG, CG)], var[:, bass.ds(g * CG, CG)],
                                        half[:, 0:CG], ALU.pow).then_inc(ln_pow, 1)

        @block.scalar
        def _(act):
            act.wait_ge(w_in, 16 * WDMAS)
            nc.scalar.activation(absw, wts[:, :], ACT.Abs).then_inc(absw_done, 1)

            def hi_1(g):
                act.wait_ge(z_scale, 1)
                act.wait_ge(z_mm, g + 1)
                nc.scalar.activation(z_hi[:, 0, CG * g:CG * g + CG, :], work[:, g, :].rearrange(
                    "p (c f) -> p c f", c=CG), ACT.Copy, scale=zmul[:, 1:2]).then_inc(z_act, 1)

            def row_sums(b, s):
                nc.scalar.activation(junk, ring[:, s, :], ACT.Abs,
                                     accum_out=rowsum[:, bass.ds(b, 1)]).then_inc(abs_done, 1)


            def hT_copy(g):
                act.wait_ge(hT_mm, g + 1)
                nc.scalar.activation(*hT_places(g), ACT.Relu).then_inc(hT_done, 1)

            act.wait_ge(ln_ready, 1)
            for k in range(CG):
                last = nc.scalar.activation(h_ln[:, k, :], xs[:, k, :], ACT.Identity, scale=rstd[:, k:k + 1],
                                            bias=nbias[:, k:k + 1])
            last.then_inc(h_first, 1)
            hT_copy(0)
            hT_copy(1)
            act.wait_ge(row_in[0], 16)
            row_sums(0, 0)
            act.wait_ge(row_in[1], 16)
            act.wait_ge(abs_done, 1)
            row_sums(1, 1)
            hT_copy(2)
            hi_1(0)
            hT_copy(3)
            hi_1(1)
            hi_1(2)
            hi_1(3)

            def adjacency_group(g, first=False, last=False):
                for s in range(CG):
                    t = (s + 1) % CG

                    def sums_ahead():
                        act.wait_ge(row_in[t], g * 16 + (16 if t else 32))
                        act.wait_ge(abs_done, g * CG + (s + 1))
                        row_sums(g * CG + (s + 1), t)

                    if not (first and s < 2) and not (last and t == 0):
                        sums_ahead()
                    act.wait_ge(a_scale, g * CG + (s + 1))
                    for q in range(4):
                        act.wait_ge(t_mm, g * 16 + (4 * s + q + 1))
                        nc.scalar.activation(at_hi[:, 4 * q:4 * q + 4, bass.ds(g * IT + s * P, P)],
                                             work[:, q, :].rearrange("p (c f) -> p c f", c=4), ACT.Copy,
                                             scale=ascale[:, bass.ds(g * CG + s, 1)]).then_inc(a_hi, 1)
                    if first and s == 1:
                        sums_ahead()

            adjacency_group(0, first=True)
            with act.Fori(1, G - 1) as g:
                adjacency_group(g)
            adjacency_group(G - 1, last=True)

            def z_bank(l, it, width):
                b = work[:, 0, :] if l == 5 else acc[:, bass.ds(it * IT, CG * width)]
                return b.rearrange("p (c f) -> p c f", c=CG)

            def hi(l, it, width, relu=False):
                act.wait_ge(z_mm, it + (4 * l + 1))
                if relu:
                    act.wait_ge(z_split, it + 4 * l)
                    nc.scalar.activation(tmp[:, :, 0:Q], z_bank(l, it, Q), ACT.Relu, scale=zmul[:, l + 1:l + 2]).then_inc(z_act, 1)
                else:
                    nc.scalar.activation(z_hi[:, l % 2, bass.ds(it * CG, CG), 0:width],
                                         z_bank(l, it, width), ACT.Copy,
                                         scale=zmul[:, l + 1:l + 2]).then_inc(z_act, 1)

            for l in range(1, 6):
                act.wait_ge(z_scale, l + 1)
                with act.Fori(0, G) as it:
                    if l == 4:
                        act.wait_ge(mid_mm, it + 1)
                        nc.scalar.activation(zT[:, :], work[:, it, :], ACT.Relu).then_inc(mid_relu, 1)
                    hi(l, it, Q if l == 2 else P, relu=l == 3)
            with act.Fori(0, G) as it:
                act.wait_ge(ln_ready, it + (G + 1))
                act.wait_ge(z_split, it + 4 * 6)
                for c in range(CG):
                    k = it * CG + c
                    last = nc.scalar.activation(tmp[:, c, :], xs[:, k, :], ACT.Relu, scale=rstd[:, bass.ds(k, 1)],
                                                bias=nbias[:, bass.ds(k, 1)])
                last.then_inc(z_act, 1)
            act.wait_ge(z_split, 4 * 7)

            def result_relu(it):
                act.wait_ge(gw_mm, it * CG + 1)
                for c in range(CG):
                    if c:
                        act.wait_ge(gw_mm, it * CG + (c + 1))
                    nc.scalar.activation(tmp[:, c, :], last4[c], ACT.Relu,
                                         scale=dO[:, bass.ds(it * CG + c, 1)]).then_inc(o_relu, 1)

            result_relu(0)
            with act.Fori(1, G) as it:
                act.wait_ge(o_done, it * CG)
                result_relu(it)

        @block.vector
        def _(dve):
            steps = [0]

            def step(ins):
                steps[0] += 1
                ins.then_inc(dve_step, 1)
                dve.wait_ge(dve_step, steps[0])

            def loop_step(ins, i, per, n):
                if per == 0:
                    step(ins)
                    return
                ins.then_inc(dve_step, 1)
                dve.wait_ge(dve_step, i * per + (steps[0] + n))

            def scale_of(l, bound, target=TO_HALF):
                step(nc.vector.tensor_scalar(bnd[:, l:l + 1], bound, TINY, target, ALU.max, ALU.mult))
                step(nc.vector.tensor_scalar(zinv[:, l:l + 1].bitcast(I32), bnd[:, l:l + 1].bitcast(I32), EXPONENT,
                                             None, ALU.bitwise_and))
                step(nc.vector.reciprocal(zmul[:, l:l + 1], zinv[:, l:l + 1]))

            dve.wait_ge(consts, 3)
            nc.vector.tensor_copy(eye16[:, :], eye[:, :]).then_inc(eyes, 1)
            nc.vector.tensor_copy(ones16[:, :], ones[:, 0:1]).then_inc(eyes, 1)
            nc.vector.tensor_tensor(eye2[:, :], eye[:, 0:Q], eye[:, Q:P], ALU.add).then_inc(eyes, 1)

            def ln_stats(g):
                dve.wait_ge(x_in[g], 16)
                for c in range(CG):
                    last = nc.vector.bn_stats(stat[:, c, :], xs[:, CG * g + c, :])
                step(last)
                for c in range(CG):
                    last = nc.vector.bn_aggr(mv[:, CG * g + c, :], stat[:, c, :])
                step(last)
                c = slice(CG * g, CG * g + CG)
                nc.vector.tensor_scalar(t16[:, c], mv[:, c, 0], -1.0, None, ALU.mult)
                nc.vector.tensor_scalar(var[:, c], mv[:, c, 1], EPS, None, ALU.add).then_inc(ln_var, 1)

            def ln_apply(g):
                dve.wait_ge(ln_ready, g + 1)
                for k in range(CG * g, CG * g + CG):
                    last = nc.vector.tensor_scalar(h_ln[:, k, :], xs[:, k, :], rstd[:, k:k + 1], nbias[:, k:k + 1],
                                                   ALU.mult, ALU.add)
                last.then_inc(h_done, 1)

            def lo_1(g):
                dve.wait_ge(z_act, g + 1)
                c = slice(CG * g, CG * g + CG)
                nc.vector.scalar_tensor_tensor(
                    out=z_lo[:, 0, c, :], in0=work[:, g, :].rearrange("p (c f) -> p c f", c=CG),
                    scalar=zmul[:, 1:2], in1=z_hi[:, 0, c, :], op0=ALU.mult,
                    op1=ALU.subtract).then_inc(z_split, 1)

            ln_stats(0)
            ln_stats(1)
            ln_stats(2)
            dve.wait_ge(norm_mm, 1)
            nc.vector.tensor_reduce(cnorm[:, 4:5], work[:, 2, 0:P], AX.X, ALU.max).then_inc(norm_read, 1)
            ln_apply(1)
            ln_stats(3)
            ln_apply(2)
            ln_apply(3)
            for l, src in ((1, work[:, 3, 0:P]), (2, work[:, 3, P:2 * P]), (3, work[:, 3, 2 * P:2 * P + Q]),
                           (5, work[:, 3, 2 * P + Q:3 * P + Q])):
                last = nc.vector.tensor_reduce(cnorm[:, l:l + 1], src, AX.X, ALU.max)
            step(last)
            step(nc.vector.tensor_scalar(bnd[:, 0:1], cnorm[:, 1:2], LN_BOUND, None, ALU.mult))
            scale_of(1, bnd[:, 0:1])
            nc.vector.tensor_copy(bnd[:, 7:8], bnd[:, 0:1]).then_inc(z_scale, 1)

            def z1_maximum(h):
                nc.vector.tensor_reduce(zmax[:, 0:1] if h == 0 else zmax[:, 7:8],
                                        z_hi[:, 0, h * NC // 2:(h + 1) * NC // 2, :], AX.XY, ALU.max,
                                        apply_absolute_value=True).then_inc(zmax1, 1)

            def z_maximum(l, width):
                nc.vector.tensor_reduce(zmax[:, l:l + 1], z_hi[:, (l - 1) % 2, :, 0:width], AX.XY, ALU.max,
                                        apply_absolute_value=True).then_inc(zmax_done, 1)

            def block_scale(b, i, per, n=1):
                c = bass.ds(b, 1)
                dve.wait_ge(max_done, b + 1)
                loop_step(nc.vector.tensor_scalar(t16[:, c], rowmax[:, c], TINY, TO_HALF, ALU.max, ALU.mult), i, per,
                          2 * n - 1)
                loop_step(nc.vector.tensor_scalar(ainv[:, c].bitcast(I32), t16[:, c].bitcast(I32), EXPONENT, None,
                                                  ALU.bitwise_and), i, per, 2 * n)
                nc.vector.reciprocal(ascale[:, c], ainv[:, c]).then_inc(a_scale, 1)

            def low_halves(b, after=None, then=None):
                dve.wait_ge(a_scale, b + 1)
                for q in range(4):
                    dve.wait_ge(a_hi, b * 4 + (q + 1))
                    at = bass.ds(b * P, P)
                    nc.vector.scalar_tensor_tensor(
                        out=at_lo[:, 4 * q:4 * q + 4, at], in0=work[:, q, :].rearrange("p (c f) -> p c f", c=4),
                        scalar=ascale[:, bass.ds(b, 1)], in1=at_hi[:, 4 * q:4 * q + 4, at], op0=ALU.mult,
                        op1=ALU.subtract).then_inc(a_lo, 1)
                    if q == after:
                        then()

            def off_scales(dst, it, table, relu=False):
                t = table.unsqueeze(2).to_broadcast([P, CG, P])
                src = acc[:, bass.ds(it * IT, IT)].rearrange("p (c n) -> p c n", c=CG)
                d = dst[:, :].rearrange("p (c n) -> p c n", c=CG)
                if relu:
                    return nc.vector.scalar_tensor_tensor(out=d, in0=src, scalar=0.0, in1=t, op0=ALU.max,
                                                          op1=ALU.mult)
                return nc.vector.tensor_tensor(d, src, t, ALU.mult)

            def evacuate(l, it, relu):
                dve.wait_ge(acc_done, it + (4 * (l - 1) + 1))
                table = ainv[:, bass.ds(it * CG, CG)] if l == 1 else tab[:, l, bass.ds(it * CG, CG)]
                off_scales(pT if l in (4, 6) else zT, it, table, relu).then_inc(t_ready, 1)

            def lo(l, it, width):
                dve.wait_ge(z_act, it + (4 * l + 1))
                c = bass.ds(it * CG, CG)
                if width == P:
                    dst = z_lo[:, l % 2, c, :]
                else:
                    dst = z_hi[:, l % 2, c, Q:P]
                src = work[:, 0, :] if l == 5 else acc[:, bass.ds(it * IT, CG * width)]
                nc.vector.scalar_tensor_tensor(
                    out=dst, in0=src.rearrange("p (c f) -> p c f", c=CG),
                    scalar=zmul[:, l + 1:l + 2], in1=z_hi[:, l % 2, c, 0:width], op0=ALU.mult,
                    op1=ALU.subtract).then_inc(z_split, 1)

            def take_scale(l):
                step(nc.vector.tensor_scalar(zinv[:, l:l + 1].bitcast(I32), bnd[:, l:l + 1].bitcast(I32), EXPONENT,
                                             None, ALU.bitwise_and))
                last = nc.vector.reciprocal(zmul[:, l:l + 1], zinv[:, l:l + 1])
                if l == 2:
                    step(last)
                    last = nc.vector.tensor_tensor(zmul[:, 2:3], zmul[:, 2:3], zinv[:, 1:2], ALU.mult)
                last.then_inc(z_scale, 1)
                step(nc.vector.tensor_scalar(tab[:, l, :], ainv[:, :], zinv[:, l:l + 1], None, ALU.mult))

            def next_scale(l):
                step(nc.vector.tensor_tensor(K[:, l + 1:l + 2], K[:, l + 1:l + 2], zinv[:, l:l + 1], ALU.mult))
                dve.wait_ge(gmax_done, l)
                step(nc.vector.tensor_scalar(bnd[:, l + 1:l + 2], gmax[:, l:l + 1], K[:, l + 1:l + 2], TINY * TO_HALF,
                                             ALU.mult, ALU.max))
                take_scale(l + 1)

            def sum_chunk(j, done):
                for n, part in enumerate((at_hi, at_lo)):
                    dve.wait_ge(deg_dve, done + n)
                    nc.vector.tensor_tensor(S[:, N // 2:N], S[:, N // 2:N], part[:, j, N // 2:N],
                                            ALU.add).then_inc(deg_dve, 1)

            def first_bound():
                dve.wait_ge(gmax_done, 1)
                step(nc.vector.tensor_scalar(K[:, 2:3], cnorm[:, 2:3], zinv[:, 1:2], TO_HALF, ALU.mult, ALU.mult))
                step(nc.vector.tensor_scalar(K[:, 2:3], K[:, 2:3], gmax[:, 1:2], None, ALU.mult))

            def bounds():
                dve.wait_ge(max_done, NC)
                step(nc.vector.tensor_reduce(R[:, :], rowmax[:, :], AX.X, ALU.max))
                step(nc.vector.tensor_scalar(bnd[:, 2:3], R[:, 0:1], K[:, 2:3], TINY * TO_HALF, ALU.mult, ALU.max))
                take_scale(2)
                nc.vector.tensor_scalar(K[:, 3:4], cnorm[:, 3:4], R[:, 0:1], TO_HALF, ALU.mult, ALU.mult)
                nc.vector.tensor_scalar(K[:, 4:5], R[:, :], TO_HALF, None, ALU.mult)
                nc.vector.tensor_scalar(K[:, 6:7], R[:, :], TO_HALF, None, ALU.mult)
                step(nc.vector.tensor_scalar(K[:, 5:6], cnorm[:, 5:6], R[:, 0:1], TO_HALF, ALU.mult, ALU.mult))
                step(nc.vector.tensor_scalar(K[:, 5:6], K[:, 5:6], cnorm[:, 4:5], None, ALU.mult))

            lo_1(0)
            lo_1(1)
            block_scale(0, 0, 0)
            z1_maximum(0)
            lo_1(2)
            lo_1(3)
            low_halves(0, 0, lambda: block_scale(1, 0, 0))
            low_halves(1)
            block_scale(2, 0, 0)
            low_halves(2, 2, lambda: block_scale(3, 0, 0))
            low_halves(3, 2, lambda: block_scale(4, 0, 0))
            z1_maximum(1)
            dve.wait_ge(zmax1, 2)
            nc.vector.tensor_tensor(zmax[:, 1:2], zmax[:, 0:1], zmax[:, 7:8], ALU.max).then_inc(zmax_done, 1)
            with dve.Fori(1, G - 1) as g:
                for s in range(CG):
                    low_halves(g * CG + s, 2, lambda: block_scale(g * CG + (s + 1), g - 1, 2 * CG, s + 1))
                    if s == 1:
                        evacuate(1, g - 1, True)
            steps[0] += 2 * CG * (G - 2)
            for b in range(NC - CG, NC - 1):
                low_halves(b, 2, lambda: block_scale(b + 1, 0, 0))
                if b == NC - CG + 1:
                    evacuate(1, G - 2, True)
                    first_bound()
            bounds()
            low_halves(NC - 1)
            with dve.Fori(0, G - 1) as it:
                lo(1, it, P)
            evacuate(1, G - 1, True)
            lo(1, G - 1, P)
            dve.wait_ge(z_split, 4 * 2)

            def split(l, it):
                if l == 3:
                    dve.wait_ge(z_act, it + (4 * l + 1))
                    c = bass.ds(it * CG, CG)
                    loop_step(nc.vector.tensor_copy(z_hi[:, 1, c, 0:Q], tmp[:, :, 0:Q]), it, 1, 1)
                    nc.vector.tensor_tensor(z_hi[:, 1, c, Q:P], tmp[:, :, 0:Q], z_hi[:, 1, c, 0:Q],
                                            ALU.subtract).then_inc(z_split, 1)
                else:
                    lo(l, it, Q if l == 2 else P)

            def degrees():
                dve.wait_ge(deg_mm, NC // 2)
                step(nc.vector.tensor_tensor(t16[:, :], work[:, 3, 0:NC], ainv[:, :], ALU.mult))
                nc.vector.tensor_scalar(t16[:, :], t16[:, :], 1.0, None, ALU.add).then_inc(deg_sum, 1)

            def degree_scale():
                dve.wait_ge(deg_pow, 1)
                nc.vector.tensor_reduce(zmax[:, 7:8], dcol[:, :], AX.X, ALU.max).then_inc(zmax_done, 1)
                dve.wait_ge(gmax_done, 6)
                step(nc.vector.tensor_scalar(bnd[:, 6:7], gmax[:, 7:8], LN_BOUND, None, ALU.mult))
                scale_of(7, bnd[:, 6:7])
                nc.vector.tensor_scalar(dY[:, :], dcol[:, :], zmul[:, 7:8], None, ALU.mult)
                step(nc.vector.tensor_scalar(dO[:, :], dcol[:, :], zinv[:, 7:8], None, ALU.mult))

            for l, first, count in ((2, 1, 3), (3, 10, 1), (4, 13, 1)):
                z_maximum(l, Q if l in (3, 4) else P)
                next_scale(l)
                if l == 2:
                    nc.vector.tensor_tensor(S[:, N // 2:N], at_hi[:, 0, N // 2:N], at_lo[:, 0, N // 2:N],
                                            ALU.add).then_inc(deg_dve, 1)
                with dve.Fori(0, G - 1) as it:
                    evacuate(l, it, relu=l == 2)
                    split(l, it)
                    for k in range(count):
                        sum_chunk(it * count + (first + k), it * (2 * count) + (2 * (first + k) - 1))
                evacuate(l, G - 1, relu=l == 2)
                if l == 4:
                    dve.wait_ge(deg_pool, 2 * NC + 1)
                    dve.wait_ge(deg_dve, 2 * NC - 1)
                    nc.vector.tensor_copy(S16[:, 0, :], S[:, :]).then_inc(deg_split, 1)
                    dve.wait_ge(deg_split, 1)
                    nc.vector.tensor_tensor(S16[:, 1, :], S[:, :], S16[:, 0, :], ALU.subtract).then_inc(deg_split, 1)
                split(l, G - 1)
                if l == 3:
                    steps[0] += G
                dve.wait_ge(z_split, 4 * (l + 1))
            z_maximum(5, P)
            next_scale(5)
            for it in range(G):
                evacuate(5, it, relu=True)
                split(5, it)
                if it == 0:
                    degrees()
                if it == 1:
                    degree_scale()

            for it in range(G):
                evacuate(6, it, False)
                dve.wait_ge(z_mm, it + (4 * 6 + 1))
                c = slice(it * CG, it * CG + CG)
                nc.vector.scalar_tensor_tensor(out=xs[:, c, :], in0=work2, scalar=0.0, in1=xs[:, c, :], op0=ALU.max,
                                               op1=ALU.add).then_inc(x1_done, 1)
                dve.wait_ge(x1_done, it + 1)
                for k in range(CG):
                    last = nc.vector.bn_stats(stat[:, k, :], xs[:, it * CG + k, :])
                step(last)
                for k in range(CG):
                    last = nc.vector.bn_aggr(mv[:, it * CG + k, :], stat[:, k, :])
                step(last)
                nc.vector.tensor_scalar(var[:, c], mv[:, c, 1], EPS, None, ALU.add).then_inc(ln_var, 1)
                dve.wait_ge(ln_pow, it + (G + 1))
                step(nc.vector.tensor_tensor(rstd[:, c], rstd[:, c], dY[:, c], ALU.mult))
                nc.vector.scalar_tensor_tensor(out=nbias[:, c], in0=mv[:, c, 0], scalar=-1.0, in1=rstd[:, c],
                                               op0=ALU.mult, op1=ALU.mult).then_inc(ln_ready, 1)
                dve.wait_ge(z_act, it + (4 * 6 + 1))
                nc.vector.tensor_copy(z_hi[:, 0, c, :], tmp[:, :, 0:P])
                step(nc.vector.tensor_copy(y1[:, 0, c, :], tmp[:, :, P:D]))
                nc.vector.tensor_tensor(z_lo[:, 0, c, :], tmp[:, :, 0:P], z_hi[:, 0, c, :], ALU.subtract)
                nc.vector.tensor_tensor(y1[:, 1, c, :], tmp[:, :, P:D], y1[:, 0, c, :],
                                        ALU.subtract).then_inc(z_split, 1)

            with dve.Fori(0, G) as it:
                for h, dst in enumerate((pT, zT)):
                    dve.wait_ge(acc_done, it * 2 + (4 * 6 + h + 1))
                    t = ainv[:, bass.ds(it * CG, CG)].unsqueeze(2).to_broadcast([P, CG, P])
                    loop_step(nc.vector.tensor_tensor(
                        dst[:, :].rearrange("p (c n) -> p c n", c=CG),
                        acc[:, h * IT:(h + 1) * IT].rearrange("p (c n) -> p c n", c=CG), t, ALU.mult), it, 2, h + 1)
                    dve.wait_ge(yt_mm, it + 1)
                    nc.vector.tensor_tensor(dst[:, :], dst[:, :], work[:, h, :], ALU.add).then_inc(t_ready, 1)
                for c in range(CG):
                    dve.wait_ge(o_relu, it * CG + (c + 1))
                    k = it * CG + c
                    nc.vector.tensor_tensor(xs[:, k, :], xs[:, k, :], tmp[:, c, :], ALU.add).then_inc(o_done, 1)

        @block.tensor
        def _(pe):
            def keep_warm(n, bank):
                for _ in range(n):
                    nc.tensor.matmul(work[:, bank, 0:P], ones[:, :], ones[:, :], start=True, stop=True)

            pe.wait_ge(consts, 3)
            keep_warm(WARM[0], 0)
            pe.wait_ge(absw_done, 1)
            nc.tensor.matmul(work[:, 3, 0:P], ones[:, :], absw[:, 0:P], start=True, stop=False)
            nc.tensor.matmul(work[:, 3, 0:P], ones[:, :], absw[:, P:2 * P], start=False, stop=True)
            nc.tensor.matmul(work[:, 3, P:3 * P + Q], ones[:, :], absw[:, 2 * P:4 * P + Q], start=True, stop=True)
            nc.tensor.matmul(work[:, 2, 0:P], ones[0:Q, :], absw[0:Q, 4 * P + Q:5 * P + Q], start=True,
                             stop=True).then_inc(norm_mm, 1)

            def ln_transposes(g):
                if g == 0:
                    pe.wait_ge(h_first, 1)
                else:
                    pe.wait_ge(h_done, g)
                if g >= 2:
                    pe.wait_ge(hT_done, g - 1)
                for c in range(CG):
                    for h in range(2):
                        n = (g % 2) * 2 * IT + (2 * c + h) * P
                        last = nc.tensor.transpose(acc[:, n:n + P], h_ln[:, CG * g + c, h * P:(h + 1) * P], eye[:, :])
                last.then_inc(hT_mm, 1)

            def first_z(g):
                pe.wait_ge(hT_done, g + 1)
                if g == 2:
                    pe.wait_ge(norm_read, 1)
                if g == 3:
                    pe.wait_ge(z_scale, 1)
                for c in range(CG):
                    for h in range(2):
                        last = nc.tensor.matmul(work[:, g, c * P:(c + 1) * P], hT[:, CG * g + c, h * P:(h + 1) * P], W1[:, h, :],
                                                start=h == 0, stop=h == 1)
                last.then_inc(z_mm, 1)

            keep_warm(WARM[1], 0)
            ln_transposes(0)
            keep_warm(WARM[2], 0)
            ln_transposes(1)
            first_z(0)
            first_z(1)
            ln_transposes(2)
            ln_transposes(3)
            first_z(2)
            first_z(3)

            def transposes(g, s, q):
                if q == 0:
                    pe.wait_ge(row_in[s], g * 16 + 16)
                for k in range(4):
                    n = (4 * q + k) * P
                    last = nc.tensor.transpose(work[:, q, k * P:(k + 1) * P], ring[:, s, n:n + P], eye[:, :])
                last.then_inc(t_mm, 1)

            for s in range(2):
                for q in range(4):
                    if s == 0:
                        pe.wait_ge(z_split, q + 1)
                    else:
                        pe.wait_ge(a_lo, 4 * (s - 1) + q + 1)
                    transposes(0, s, q)

            def products(l, out_, j, i, first=False, last=False, n=IT):
                if l == 7:
                    zh, zl = z_hi[:, 0, j, :], z_lo[:, 0, j, :]
                elif l == 8:
                    zh, zl = y1[:, 0, j, :], y1[:, 1, j, :]
                else:
                    zh, zl = z_hi[:, (l - 1) % 2, j, :], z_lo[:, (l - 1) % 2, j, :]
                a, b = at_hi[:, j, bass.ds(i, n)], at_lo[:, j, bass.ds(i, n)]
                nc.tensor.matmul(out_, zh, b, start=first, stop=False)
                if l in (3, 4):
                    return nc.tensor.matmul(out_, zh, a, start=False, stop=last)
                nc.tensor.matmul(out_, zl, a, start=False, stop=False)
                return nc.tensor.matmul(out_, zh, a, start=False, stop=last)

            def unit(l, out_, i, slot_a=None, slot_b=None, z_count=None, after=None, js=range(NC)):
                slots = {3 if l in (3, 4, 7) else 2: slot_a, 7: slot_b}
                for j in js:
                    if z_count and j % CG == 0:
                        pe.wait_ge(z_split, z_count + j // CG)
                    if slots.get(j):
                        slots[j]()
                    done = products(l, out_, j, i, first=j == 0, last=j == NC - 1)
                    if after and j >= NC // 2:
                        after(j)
                if js[-1] == NC - 1:
                    done.then_inc(acc_done, 1)

            def bank(it):
                return acc[:, bass.ds(it * IT, IT)]

            def to_nodes(l, it, w, width):
                pe.wait_ge(t_ready, it + (4 * (l - 1) + 1))
                for c in range(CG):
                    last = nc.tensor.matmul(acc[:, bass.ds(it * IT + c * width, width)], zT[:, c * P:(c + 1) * P], w,
                                            start=True, stop=True)
                last.then_inc(z_mm, 1)

            def small_a(l, it):
                if l == 1:
                    to_nodes(1, it, W2, H)
                elif l == 2:
                    to_nodes(2, it, W3, Q)
                elif l == 3:
                    to_nodes(3, it, eye2[:, :], Q)
                elif l == 4:
                    pe.wait_ge(t_ready, it + (4 * 3 + 1))
                    nc.tensor.matmul(work[:, it, :], W4, pT[:, :], start=True, stop=True).then_inc(mid_mm, 1)
                elif l == 5:
                    pe.wait_ge(t_ready, it + (4 * 4 + 1))
                    pe.wait_ge(z_split, it + 4 * 5)
                    for c in range(CG):
                        last = nc.tensor.transpose(work[:, 0, c * P:(c + 1) * P], zT[:, c * P:(c + 1) * P], eye[:, :])
                    last.then_inc(z_mm, 1)
                elif l == 6:
                    pe.wait_ge(t_ready, it + (4 * 5 + 1))
                    for c in range(CG):
                        last = nc.tensor.matmul(work2[:, c, :], pT[:, c * P:(c + 1) * P], w6s[:, :], start=True,
                                                stop=True)
                    last.then_inc(z_mm, 1)

            def small_b(l, it):
                if l == 4:
                    pe.wait_ge(mid_relu, it + 1)
                    for c in range(CG):
                        last = nc.tensor.matmul(acc[:, bass.ds(it * IT + c * P, P)], zT[:, c * P:(c + 1) * P], W5,
                                                start=True, stop=True)
                    last.then_inc(z_mm, 1)

            def first_layer_unit(g, small=True, last=False):
                for h in range(2):
                    for j in range(NC):
                        if j % 4 == 0:
                            pe.wait_ge(a_lo, g * 16 + (8 * h + 5 + j // 4))
                        done = products(1, acc[:, bass.ds(g * IT + h * IT // 2, IT // 2)], j, g * IT + h * IT // 2,
                                        first=j == 0, last=j == NC - 1, n=IT // 2)
                        if j % 2 == 1 and not (last and h == 1):
                            k = 8 * (h + 1) + j // 2
                            pe.wait_ge(a_lo, g * 16 + (k - 3))
                            transposes(g + k // 16, k // 4 % CG, k % 4)
                        if small and h == 1 and j == 2:
                            small_a(1, g - 1)
                done.then_inc(acc_done, 1)

            pe.wait_ge(z_split, 4)
            first_layer_unit(0, small=False)
            with pe.Fori(1, G - 1) as g:
                first_layer_unit(g)
            first_layer_unit(G - 1, last=True)

            def degree_sums(j):
                if j == NC // 2:
                    pe.wait_ge(deg_split, 2)
                for c in (2 * j - NC, 2 * j - NC + 1):
                    for n in range(2):
                        last = nc.tensor.matmul(work[:, 3, c:c + 1], S16[:, n, c * P:(c + 1) * P], ones16[:, :],
                                                start=n == 0, stop=n == 1)
                last.then_inc(deg_mm, 1)

            def slots(l, it):
                return {"slot_a": lambda: small_a(l, it), "slot_b": lambda: small_b(l, it)}

            for l in range(2, 7):
                unit(l, bank(0), 0, **slots(l - 1, G - 1), z_count=4 * (l - 1) + 1,
                     after=degree_sums if l == 5 else None)
                if l < 6:
                    with pe.Fori(1, G) as it:
                        unit(l, bank(it), it * IT, **slots(l, it - 1))
            pe.wait_ge(w_late, 32)
            unit(6, bank(1), IT, **slots(6, 0))
            with pe.Fori(2, G) as it:
                pe.wait_ge(x1_done, it - 1)
                unit(6, bank(it), it * IT, **slots(6, it - 1))

            def y_transposed(it):
                for h in range(2):
                    for c in range(CG):
                        j = it * CG + c
                        zh, zl = (z_hi[:, 0, j, :], z_lo[:, 0, j, :]) if h == 0 else (y1[:, 0, j, :], y1[:, 1, j, :])
                        o = work[:, h, c * P:(c + 1) * P]
                        nc.tensor.matmul(o, zl, eye16[:, :], start=True, stop=False)
                        last = nc.tensor.matmul(o, zh, eye16[:, :], start=False, stop=True)
                last.then_inc(yt_mm, 1)

            def last_product(it, h):
                pe.wait_ge(t_ready, it * 2 + (4 * 6 + 1 + h))
                if h == 0:
                    with_previous = it * CG
                    if not (type(it) is int and it == 0):
                        pe.wait_ge(o_relu, with_previous)
                for c in range(CG):
                    done = nc.tensor.matmul(last4[c], (pT, zT)[h][:, c * P:(c + 1) * P], w7s[:, h, :], start=h == 0,
                                            stop=h == 1)
                    if h == 1:
                        done.then_inc(gw_mm, 1)

            def last_small():
                pe.wait_ge(x1_done, G - 1)
                small_a(6, G - 1)

            pe.wait_ge(eyes, 3)
            early, late = range(12), range(12, NC)
            unit(7, bank(0), 0, slot_a=last_small, z_count=4 * 6 + 1, js=early)
            unit(8, bank(1), 0, js=early)
            pe.wait_ge(x1_done, G)
            y_transposed(0)
            pe.wait_ge(z_split, 4 * 7)
            unit(7, bank(0), 0, js=late)
            unit(8, bank(1), 0, js=late)
            pe.wait_ge(w_late, 32)
            pe.wait_ge(t_ready, 4 * 6 + 1)
            last_product(0, 0)
            with pe.Fori(1, G) as it:
                unit(7, bank(0), it * IT, slot_a=lambda: last_product(it - 1, 1))
                unit(8, bank(1), it * IT, slot_a=lambda: y_transposed(it), slot_b=lambda: last_product(it, 0))
            last_product(G - 1, 1)


_INS = ["x", "adj", "L0_gnn_W1", "L0_gnn_W2", "L0_gnn_W3", "L0_gnn_W4", "L0_gnn_W5", "L0_gnn_W6", "L1_gnn_W"]


def kernel(**inputs):
    import numpy as _np
    import concourse.bacc as _bacc
    from concourse import mybir as _mybir
    from concourse.bass_utils import run_bass_kernel_spmd as _run

    nc = _bacc.Bacc("TRN2", target_bir_lowering=False, num_devices=1)
    arrays, args = {}, []
    for name in _INS:
        a = _np.ascontiguousarray(inputs[name])
        arrays[f"in_{name}"] = a
        args.append(nc.dram_tensor(f"in_{name}", a.shape, _mybir.dt.from_np(a.dtype), kind="ExternalInput").ap())
    out = nc.dram_tensor("out", arrays["in_x"].shape, _mybir.dt.float32, kind="ExternalOutput").ap()
    adjacency_net(nc, *args, out)
    return _run(nc, [arrays], core_ids=[0]).results[0]["out"]
```

```python
from contextlib import ExitStack

import concourse.bass as bass
from concourse import mybir

P = 128
F32 = mybir.dt.float32
F16 = mybir.dt.float16
I32 = mybir.dt.int32
ALU = mybir.AluOpType
ACT = mybir.ActivationFunctionType
AX = mybir.AxisListType
RMAX = bass.bass_isa.ReduceOp.max

EXPONENT = 0x7F800000
TINY = 1e-30
TO_HALF = 2.0 ** -14
EPS = 1e-5


def adjacency_net(nc, x, adj, w1, w2, w3, w4, w5, w6, w7, out):
    N, D = x.shape
    NC = N // P
    H = w1.shape[1]
    Q = w3.shape[1]
    IT = 512
    G = N // IT
    CG = IT // P
    LN_BOUND = float(D) ** 0.5
    assert D == 2 * P and H == P and 2 * Q == P and NC == G * CG

    x_v = x.rearrange("(c p) f -> p c f", p=P)
    out_v = out.rearrange("(c p) f -> p c f", p=P)

    with ExitStack() as ctx:
        def sb(name, shape, dt):
            return ctx.enter_context(nc.sbuf_tensor(name, shape, dt))

        def sem(name):
            return ctx.enter_context(nc.semaphore(name))

        at_hi = sb("at_hi", [P, NC, N], F16)
        at_lo = sb("at_lo", [P, NC, N], F16)
        ring = sb("ring", [P, CG, N], F32)
        xs = sb("xs", [P, NC, D], F32)
        z_hi = sb("z_hi", [P, 2, NC, P], F16)
        z_lo = sb("z_lo", [P, 2, NC, P], F16)
        wts = sb("wts", [P, 5 * P + Q], F32)
        w6s = sb("w6s", [P, D], F32)
        w7s = sb("w7s", [P, 2, D], F32)
        zT = sb("zT", [P, IT], F32)
        eye = sb("eye", [P, P], F32)
        eye16 = sb("eye16", [P, P], F16)
        eye2 = sb("eye2", [P, Q], F32)
        ones = sb("ones", [P, P], F32)
        ones16 = sb("ones16", [P, 1], F16)
        stat = sb("stat", [P, CG, 6], F32)
        mv = sb("mv", [P, NC, 2], F32)
        var = sb("var", [P, NC], F32)
        half = sb("half", [P, NC], F32)
        rstd = sb("rstd", [P, NC], F32)
        nbias = sb("nbias", [P, NC], F32)
        rowsum = sb("rowsum", [P, NC], F32)
        sums4 = sb("sums4", [P, 4], F32)
        rowmax = sb("rowmax", [P, NC], F32)
        t16 = sb("t16", [P, NC], F32)
        ainv = sb("ainv", [P, NC], F32)
        ascale = sb("ascale", [P, NC], F32)
        cnorm = sb("cnorm", [P, 8], F32)
        R = sb("R", [P, 1], F32)
        K = sb("K", [P, 8], F32)
        zmax = sb("zmax", [P, 8], F32)
        gmax = sb("gmax", [P, 8], F32)
        bnd = sb("bnd", [P, 8], F32)
        zinv = sb("zinv", [P, 8], F32)
        zmul = sb("zmul", [P, 8], F32)
        tab = sb("tab", [P, 8, NC], F32)
        dcol = sb("dcol", [P, NC], F32)
        dY = sb("dY", [P, NC], F32)
        dO = sb("dO", [P, NC], F32)
        wmax = sb("wmax", [P, 2], F32)
        wall = sb("wall", [P, 2], F32)
        winv = sb("winv", [P, 2], F32)
        wmul = sb("wmul", [P, 2], F32)
        ginv = sb("ginv", [P, 1], F32)
        gmul = sb("gmul", [P, 1], F32)
        s6 = sb("s6", [P, 1], F32)

        W1 = wts[:, 0:2 * P].rearrange("p (h n) -> p h n", h=2)
        W2 = wts[:, 2 * P:3 * P]
        W3 = wts[:, 3 * P:3 * P + Q]
        W5 = wts[:, 3 * P + Q:4 * P + Q]
        W4 = wts[:, 4 * P + Q:5 * P + Q]
        h_ln = at_lo[:, :, N - IT:N].bitcast(F32)
        hT = at_hi[:, :, N - IT:N].bitcast(F32)
        absw = z_hi[:, 1, :, :].rearrange("p c f -> p (c f)").bitcast(F32)[:, 0:5 * P + Q]
        S = ring[:, 0, :]
        slot3 = ring[:, 3, :].bitcast(F16)
        S16 = slot3.rearrange("p (s n) -> p s n", s=2)
        w7_halves = slot3[:, 0:4 * D].rearrange("p (s h n) -> p s h n", s=2, h=2)
        w6_halves = slot3[:, 4 * D:6 * D].rearrange("p (s n) -> p s n", s=2)
        x6 = ring[:, 0, 0:CG * D].rearrange("p (c f) -> p c f", c=CG)
        pT = ring[:, 1, 0:IT]
        gsrc = (pT, zT[:, :])
        gT = slot3[:, 6 * D:6 * D + 4 * IT].rearrange("p (h s n) -> p h s n", h=2, s=2)
        tmp = ring[:, 1, IT:IT + CG * D].rearrange("p (c f) -> p c f", c=CG)
        y1 = ring[:, 2, :].bitcast(F16).rearrange("p (s c f) -> p s c f", s=2, c=NC)
        junk = z_lo[:, 1, :, :].rearrange("p c f -> p (c f)")

        acc = ctx.enter_context(nc.psum_tensor("acc", [P, G * IT], F32))
        work = ctx.enter_context(nc.psum_tensor("work", [P, G, IT], F32))
        work2 = work[:, 0:2, :].rearrange("p b n -> p (b n)").rearrange("p (c f) -> p c f", c=CG)
        last4 = [acc[:, 2 * IT:2 * IT + D], acc[:, 3 * IT:3 * IT + D], work[:, 2, 0:D], work[:, 3, 0:D]]

        x_in = [sem(f"x_in{g}") for g in range(G)]
        row_in = [sem(f"row_in{s}") for s in range(CG)]
        w_in = sem("w_in")
        w_late = sem("w_late")
        consts = sem("consts")
        eyes = sem("eyes")
        absw_done = sem("absw_done")
        norm_mm = sem("norm_mm")
        norm_read = sem("norm_read")
        dve_step = sem("dve_step")
        pool_step = sem("pool_step")
        ln_var = sem("ln_var")
        ln_pow = sem("ln_pow")
        ln_ready = sem("ln_ready")
        h_first = sem("h_first")
        h_done = sem("h_done")
        hT_mm = sem("hT_mm")
        hT_done = sem("hT_done")
        z_mm = sem("z_mm")
        z_act = sem("z_act")
        z_split = sem("z_split")
        abs_done = sem("abs_done")
        dve_sums = sem("dve_sums")
        max_done = sem("max_done")
        a_scale = sem("a_scale")
        t_mm = sem("t_mm")
        a_hi = sem("a_hi")
        a_lo = sem("a_lo")
        acc_done = sem("acc_done")
        t_ready = sem("t_ready")
        z_scale = sem("z_scale")
        zmax1 = sem("zmax1")
        zmax_done = sem("zmax_done")
        gmax_done = sem("gmax_done")
        mid_mm = sem("mid_mm")
        mid_relu = sem("mid_relu")
        deg_dve = sem("deg_dve")
        deg_pool = sem("deg_pool")
        deg_split = sem("deg_split")
        deg_mm = sem("deg_mm")
        deg_sum = sem("deg_sum")
        deg_pow = sem("deg_pow")
        wmax_done = sem("wmax_done")
        w_split = sem("w_split")
        g_hi = sem("g_hi")
        g_split = sem("g_split")
        x_relu = sem("x_relu")
        x1_done = sem("x1_done")
        yt_mm = sem("yt_mm")
        gw_mm = sem("gw_mm")
        o_relu = sem("o_relu")
        o_done = sem("o_done")
        stored = sem("stored")

        W_LOADS = 6
        WARM = (12, 5, 2)
        block = ctx.enter_context(nc.Block())

        def hT_places(g):
            return (hT[:, CG * g:CG * g + CG, :],
                    acc[:, (g % 2) * 2 * IT:(g % 2 + 1) * 2 * IT].rearrange("p (c n) -> p c n", c=CG))

        @block.sync
        def _(sp):
            def load_x(g):
                sp.dma_start(xs[:, CG * g:CG * g + CG, :], x_v[:, CG * g:CG * g + CG, :]).then_inc(x_in[g], 16)

            load_x(0)
            load_x(1)
            for dst, src in ((W1, w1.rearrange("(h p) n -> p h n", p=P)), (W2, w2), (W3, w3), (W5, w5),
                             (W4[0:Q, :], w4), (W4[Q:P, :], w4)):
                sp.dma_start(dst, src).then_inc(w_in, 16)
            load_x(2)
            load_x(3)
            for s in range(CG):
                sp.dma_start(ring[:, s, :], adj[s * P:(s + 1) * P, :]).then_inc(row_in[s], 16)
            sp.dma_start(w6s[:, :], w6).then_inc(w_late, 16)
            sp.dma_start(w7s[:, :, :], w7.rearrange("(h p) n -> p h n", p=P)).then_inc(w_late, 16)
            for g in range(1, G):
                for s in range(CG):
                    sp.wait_ge(t_mm, g * 16 + (4 * s - 12))
                    sp.wait_ge(max_done, g * 4 + (s - 3))
                    sp.dma_start(ring[:, s, :], adj[g * IT + s * P:g * IT + (s + 1) * P, :]).then_inc(row_in[s], 16)
            stores = [CG * g for g in range(G)] + [NC - 2, NC - 1, NC]
            for c, d in zip(stores, stores[1:]):
                sp.wait_ge(o_done, d)
                sp.dma_start(out_v[:, c:d, :], xs[:, c:d, :]).then_inc(stored, 16)
            sp.wait_ge(stored, 16 * (len(stores) - 1))

        @block.gpsimd
        def _(pool):
            nc.gpsimd.memset(half[:, :], -0.5).then_inc(consts, 1)
            nc.gpsimd.memset(ones[:, :], 1.0).then_inc(consts, 1)
            nc.gpsimd.memset(eye[:, :], 0.0).then_inc(pool_step, 1)
            pool.wait_ge(pool_step, 1)
            nc.gpsimd.affine_select(out=eye[:, :], in_=eye[:, :], compare_op=ALU.not_equal, fill=1.0, base=0,
                                    pattern=[[-1, P]], channel_multiplier=1).then_inc(consts, 1)
            pool.wait_ge(consts, 3)
            for g in range(G):
                pool.wait_ge(ln_var, g + 1)
                c = slice(CG * g, CG * g + CG)
                nc.gpsimd.tensor_tensor(rstd[:, c], var[:, c], half[:, c], ALU.pow).then_inc(ln_pow, 1)
                pool.wait_ge(ln_pow, g + 1)
                nc.gpsimd.tensor_tensor(nbias[:, c], t16[:, c], rstd[:, c], ALU.mult).then_inc(ln_ready, 1)
            for b in range(NC):
                if b == CG - 1:
                    pool.wait_ge(dve_sums, 5)
                else:
                    pool.wait_ge(abs_done, b + 1 if b < CG - 1 else b)
                nc.gpsimd.partition_all_reduce(rowmax[:, b:b + 1], rowsum[:, b:b + 1], P,
                                               RMAX).then_inc(max_done, 1)
                if b == CG + 1:
                    pool.wait_ge(zmax_done, 1)
                    nc.gpsimd.partition_all_reduce(gmax[:, 1:2], zmax[:, 1:2], P, RMAX).then_inc(gmax_done, 1)
            pool.wait_ge(a_lo, 4 * NC)
            nc.gpsimd.memset(S[:, 0:N // 2], 0.0).then_inc(deg_pool, 1)
            for l in range(4):
                pool.wait_ge(zmax_done, l + 2)
                nc.gpsimd.partition_all_reduce(gmax[:, l + 2:l + 3], zmax[:, l + 2:l + 3], P,
                                               RMAX).then_inc(gmax_done, 1)
                if l == 0:
                    pool.wait_ge(wmax_done, 1)
                    nc.gpsimd.partition_all_reduce(wall[:, :], wmax[:, :], P, RMAX).then_inc(wmax_done, 1)
                if l == 3:
                    break
                first, count = ((0, 8), (8, 4), (12, 4))[l]
                with pool.Fori(first, first + count) as c:
                    for n, part in enumerate((at_hi, at_lo)):
                        pool.wait_ge(deg_pool, c * 2 + (n + 1))
                        nc.gpsimd.tensor_tensor(S[:, 0:N // 2], S[:, 0:N // 2], part[:, c, 0:N // 2],
                                                ALU.add).then_inc(deg_pool, 1)
            pool.wait_ge(deg_sum, 1)
            nc.gpsimd.tensor_tensor(dcol[:, :], t16[:, :], half[:, :], ALU.pow).then_inc(deg_pow, 1)
            pool.wait_ge(zmax_done, 6)
            nc.gpsimd.partition_all_reduce(gmax[:, 7:8], zmax[:, 7:8], P, RMAX).then_inc(gmax_done, 1)
            with pool.Fori(0, G) as g:
                pool.wait_ge(ln_var, g + (G + 1))
                nc.gpsimd.tensor_tensor(rstd[:, bass.ds(g * CG, CG)], var[:, bass.ds(g * CG, CG)],
                                        half[:, 0:CG], ALU.pow).then_inc(ln_pow, 1)

        @block.scalar
        def _(act):
            act.wait_ge(w_in, 16 * W_LOADS)
            nc.scalar.activation(absw, wts[:, :], ACT.Abs).then_inc(absw_done, 1)

            def hi_1(g):
                act.wait_ge(z_scale, 1)
                act.wait_ge(z_mm, g + 1)
                nc.scalar.activation(z_hi[:, 0, CG * g:CG * g + CG, :], work[:, g, :].rearrange(
                    "p (c f) -> p c f", c=CG), ACT.Copy, scale=zmul[:, 1:2]).then_inc(z_act, 1)

            def row_sums(b, s):
                nc.scalar.activation(junk, ring[:, s, :], ACT.Abs,
                                     accum_out=rowsum[:, bass.ds(b, 1)]).then_inc(abs_done, 1)

            def hT_copy(g):
                act.wait_ge(hT_mm, g + 1)
                nc.scalar.activation(*hT_places(g), ACT.Relu).then_inc(hT_done, 1)

            act.wait_ge(ln_ready, 1)
            for k in range(CG):
                last = nc.scalar.activation(h_ln[:, k, :], xs[:, k, :], ACT.Identity, scale=rstd[:, k:k + 1],
                                            bias=nbias[:, k:k + 1])
            last.then_inc(h_first, 1)
            hT_copy(0)
            hT_copy(1)
            act.wait_ge(row_in[0], 16)
            row_sums(0, 0)
            act.wait_ge(row_in[1], 16)
            act.wait_ge(abs_done, 1)
            row_sums(1, 1)
            hT_copy(2)
            hi_1(0)
            hT_copy(3)
            hi_1(1)
            hi_1(2)
            hi_1(3)

            def adjacency_group(g, first=False, last=False):
                for s in range(CG):
                    t = (s + 1) % CG

                    def sums_ahead():
                        act.wait_ge(row_in[t], g * 16 + (16 if t else 32))
                        act.wait_ge(abs_done, s + 1 if first and s < CG - 1 else g * CG + s)
                        row_sums(g * CG + (s + 1), t)

                    if not (first and s < 3) and not (last and t == 0):
                        sums_ahead()
                    act.wait_ge(a_scale, g * CG + (s + 1))
                    for q in range(4):
                        act.wait_ge(t_mm, g * 16 + (4 * s + q + 1))
                        nc.scalar.activation(at_hi[:, 4 * q:4 * q + 4, bass.ds(g * IT + s * P, P)],
                                             work[:, q, :].rearrange("p (c f) -> p c f", c=4), ACT.Copy,
                                             scale=ascale[:, bass.ds(g * CG + s, 1)]).then_inc(a_hi, 1)
                    if first and s == 1:
                        sums_ahead()

            adjacency_group(0, first=True)
            with act.Fori(1, G - 1) as g:
                adjacency_group(g)
            adjacency_group(G - 1, last=True)

            def z_bank(l, it, width):
                b = work[:, 0, :] if l == 5 else acc[:, bass.ds(it * IT, CG * width)]
                return b.rearrange("p (c f) -> p c f", c=CG)

            def hi(l, it, width, relu=False):
                act.wait_ge(z_mm, it + (4 * l + 1))
                if relu:
                    act.wait_ge(z_split, it + 4 * l)
                    nc.scalar.activation(tmp[:, :, 0:Q], z_bank(l, it, Q), ACT.Relu,
                                         scale=zmul[:, l + 1:l + 2]).then_inc(z_act, 1)
                else:
                    nc.scalar.activation(z_hi[:, l % 2, bass.ds(it * CG, CG), 0:width],
                                         z_bank(l, it, width), ACT.Copy,
                                         scale=zmul[:, l + 1:l + 2]).then_inc(z_act, 1)

            for l in range(1, 6):
                act.wait_ge(z_scale, l + 1)
                with act.Fori(0, G) as it:
                    if l == 4:
                        act.wait_ge(mid_mm, it + 1)
                        nc.scalar.activation(zT[:, :], work[:, it, :], ACT.Relu).then_inc(mid_relu, 1)
                    hi(l, it, Q if l == 2 else P, relu=l == 3)

            def g_high(h):
                nc.scalar.activation(gT[:, h, 0, :], gsrc[h], ACT.Copy).then_inc(g_hi, 1)

            act.wait_ge(deg_split, 2)
            act.wait_ge(w_split, 2)
            with act.Fori(0, G) as it:
                act.wait_ge(t_ready, it + (4 * 5 + 1))
                g_high(0)
                act.wait_ge(z_mm, it + (4 * 6 + 1))
                nc.scalar.activation(x6, work2, ACT.Relu, scale=s6[:, 0:1]).then_inc(x_relu, 1)
                act.wait_ge(ln_ready, it + (G + 1))
                act.wait_ge(z_split, it + 4 * 6)
                for c in range(CG):
                    k = it * CG + c
                    last = nc.scalar.activation(tmp[:, c, :], xs[:, k, :], ACT.Relu, scale=rstd[:, bass.ds(k, 1)],
                                                bias=nbias[:, bass.ds(k, 1)])
                last.then_inc(z_act, 1)
            act.wait_ge(z_split, 4 * 7)

            def result_relu(it):
                for c in range(CG):
                    act.wait_ge(gw_mm, it * CG + (c + 1))
                    nc.scalar.activation(tmp[:, c, :], last4[c], ACT.Relu,
                                         scale=dO[:, bass.ds(it * CG + c, 1)]).then_inc(o_relu, 1)

            for h in range(2):
                act.wait_ge(t_ready, 4 * 6 + h + 1)
                g_high(h)
            result_relu(0)
            with act.Fori(1, G - 1) as it:
                for h in range(2):
                    act.wait_ge(t_ready, it * 2 + (4 * 6 + h + 1))
                    g_high(h)
                act.wait_ge(o_done, it * CG)
                result_relu(it)
            act.wait_ge(t_ready, 4 * 6 + 2 * G - 1)
            g_high(0)
            act.wait_ge(o_done, (G - 1) * CG)
            result_relu(G - 1)

        @block.vector
        def _(dve):
            steps = [0]

            def step(ins):
                steps[0] += 1
                ins.then_inc(dve_step, 1)
                dve.wait_ge(dve_step, steps[0])

            def loop_step(ins, i, per, n):
                if per == 0:
                    step(ins)
                    return
                ins.then_inc(dve_step, 1)
                dve.wait_ge(dve_step, i * per + (steps[0] + n))

            def scale_of(l, bound, signal, count):
                step(nc.vector.tensor_scalar(bnd[:, l:l + 1], bound, TINY, TO_HALF, ALU.max, ALU.mult))
                step(nc.vector.tensor_scalar(zinv[:, l:l + 1].bitcast(I32), bnd[:, l:l + 1].bitcast(I32), EXPONENT,
                                             None, ALU.bitwise_and))
                nc.vector.reciprocal(zmul[:, l:l + 1], zinv[:, l:l + 1]).then_inc(signal, 1)
                dve.wait_ge(signal, count)

            dve.wait_ge(consts, 3)
            nc.vector.tensor_copy(eye16[:, :], eye[:, :]).then_inc(eyes, 1)
            nc.vector.tensor_copy(ones16[:, :], ones[:, 0:1]).then_inc(eyes, 1)
            nc.vector.tensor_tensor(eye2[:, :], eye[:, 0:Q], eye[:, Q:P], ALU.add).then_inc(eyes, 1)

            def ln_stats(g):
                dve.wait_ge(x_in[g], 16)
                for c in range(CG):
                    last = nc.vector.bn_stats(stat[:, c, :], xs[:, CG * g + c, :])
                step(last)
                for c in range(CG):
                    last = nc.vector.bn_aggr(mv[:, CG * g + c, :], stat[:, c, :])
                step(last)
                c = slice(CG * g, CG * g + CG)
                nc.vector.tensor_scalar(t16[:, c], mv[:, c, 0], -1.0, None, ALU.mult)
                nc.vector.tensor_scalar(var[:, c], mv[:, c, 1], EPS, None, ALU.add).then_inc(ln_var, 1)

            def ln_apply(g):
                dve.wait_ge(ln_ready, g + 1)
                for k in range(CG * g, CG * g + CG):
                    last = nc.vector.tensor_scalar(h_ln[:, k, :], xs[:, k, :], rstd[:, k:k + 1], nbias[:, k:k + 1],
                                                   ALU.mult, ALU.add)
                last.then_inc(h_done, 1)

            def lo_1(g):
                dve.wait_ge(z_act, g + 1)
                c = slice(CG * g, CG * g + CG)
                nc.vector.scalar_tensor_tensor(
                    out=z_lo[:, 0, c, :], in0=work[:, g, :].rearrange("p (c f) -> p c f", c=CG),
                    scalar=zmul[:, 1:2], in1=z_hi[:, 0, c, :], op0=ALU.mult,
                    op1=ALU.subtract).then_inc(z_split, 1)

            ln_stats(0)
            ln_stats(1)
            ln_stats(2)
            dve.wait_ge(norm_mm, 1)
            nc.vector.tensor_reduce(cnorm[:, 4:5], work[:, 2, 0:P], AX.X, ALU.max).then_inc(norm_read, 1)
            ln_apply(1)
            ln_stats(3)
            ln_apply(2)
            ln_apply(3)
            for l, src in ((1, work[:, 3, 0:P]), (2, work[:, 3, P:2 * P]), (3, work[:, 3, 2 * P:2 * P + Q]),
                           (5, work[:, 3, 2 * P + Q:3 * P + Q])):
                last = nc.vector.tensor_reduce(cnorm[:, l:l + 1], src, AX.X, ALU.max)
            step(last)
            step(nc.vector.tensor_scalar(bnd[:, 0:1], cnorm[:, 1:2], LN_BOUND, None, ALU.mult))
            scale_of(1, bnd[:, 0:1], z_scale, 1)

            def z1_maximum(h):
                nc.vector.tensor_reduce(zmax[:, 0:1] if h == 0 else zmax[:, 7:8],
                                        z_hi[:, 0, h * NC // 2:(h + 1) * NC // 2, :], AX.XY, ALU.max,
                                        apply_absolute_value=True).then_inc(zmax1, 1)

            def z_maximum(l, width):
                nc.vector.tensor_reduce(zmax[:, l:l + 1], z_hi[:, (l - 1) % 2, :, 0:width], AX.XY, ALU.max,
                                        apply_absolute_value=True).then_inc(zmax_done, 1)

            def block_scale(b, i, per, n=1):
                c = bass.ds(b, 1)
                dve.wait_ge(max_done, b + 1)
                loop_step(nc.vector.tensor_scalar(t16[:, c], rowmax[:, c], TINY, TO_HALF, ALU.max, ALU.mult), i, per,
                          2 * n - 1)
                loop_step(nc.vector.tensor_scalar(ainv[:, c].bitcast(I32), t16[:, c].bitcast(I32), EXPONENT, None,
                                                  ALU.bitwise_and), i, per, 2 * n)
                nc.vector.reciprocal(ascale[:, c], ainv[:, c]).then_inc(a_scale, 1)

            def low_halves(b, hooks={}):
                dve.wait_ge(a_scale, b + 1)
                for q in range(4):
                    dve.wait_ge(a_hi, b * 4 + (q + 1))
                    at = bass.ds(b * P, P)
                    nc.vector.scalar_tensor_tensor(
                        out=at_lo[:, 4 * q:4 * q + 4, at], in0=work[:, q, :].rearrange("p (c f) -> p c f", c=4),
                        scalar=ascale[:, bass.ds(b, 1)], in1=at_hi[:, 4 * q:4 * q + 4, at], op0=ALU.mult,
                        op1=ALU.subtract).then_inc(a_lo, 1)
                    if q in hooks:
                        hooks[q]()

            def sum_part(k):
                dve.wait_ge(row_in[CG - 1], 16)
                nc.vector.tensor_reduce(sums4[:, k:k + 1], ring[:, CG - 1, k * IT:(k + 1) * IT], AX.X, ALU.add,
                                        apply_absolute_value=True).then_inc(dve_sums, 1)
                if k == 3:
                    dve.wait_ge(dve_sums, 4)
                    nc.vector.tensor_reduce(rowsum[:, CG - 1:CG], sums4[:, :], AX.X, ALU.add).then_inc(dve_sums, 1)

            def off_scales(dst, it, table, relu=False):
                t = table.unsqueeze(2).to_broadcast([P, CG, P])
                src = acc[:, bass.ds(it * IT, IT)].rearrange("p (c n) -> p c n", c=CG)
                d = dst[:, :].rearrange("p (c n) -> p c n", c=CG)
                if relu:
                    return nc.vector.scalar_tensor_tensor(out=d, in0=src, scalar=0.0, in1=t, op0=ALU.max,
                                                          op1=ALU.mult)
                return nc.vector.tensor_tensor(d, src, t, ALU.mult)

            def evacuate(l, it, relu):
                dve.wait_ge(acc_done, it + (4 * (l - 1) + 1))
                table = ainv[:, bass.ds(it * CG, CG)] if l == 1 else tab[:, l, bass.ds(it * CG, CG)]
                off_scales(pT if l == 4 else zT, it, table, relu).then_inc(t_ready, 1)

            def lo(l, it, width):
                dve.wait_ge(z_act, it + (4 * l + 1))
                c = bass.ds(it * CG, CG)
                if width == P:
                    dst = z_lo[:, l % 2, c, :]
                else:
                    dst = z_hi[:, l % 2, c, Q:P]
                src = work[:, 0, :] if l == 5 else acc[:, bass.ds(it * IT, CG * width)]
                nc.vector.scalar_tensor_tensor(
                    out=dst, in0=src.rearrange("p (c f) -> p c f", c=CG),
                    scalar=zmul[:, l + 1:l + 2], in1=z_hi[:, l % 2, c, 0:width], op0=ALU.mult,
                    op1=ALU.subtract).then_inc(z_split, 1)

            def take_scale(l):
                step(nc.vector.tensor_scalar(zinv[:, l:l + 1].bitcast(I32), bnd[:, l:l + 1].bitcast(I32), EXPONENT,
                                             None, ALU.bitwise_and))
                last = nc.vector.reciprocal(zmul[:, l:l + 1], zinv[:, l:l + 1])
                if l == 2:
                    step(last)
                    last = nc.vector.tensor_tensor(zmul[:, 2:3], zmul[:, 2:3], zinv[:, 1:2], ALU.mult)
                last.then_inc(z_scale, 1)
                step(nc.vector.tensor_scalar(tab[:, l, :], ainv[:, :], zinv[:, l:l + 1], None, ALU.mult))

            def next_scale(l):
                step(nc.vector.tensor_tensor(K[:, l + 1:l + 2], K[:, l + 1:l + 2], zinv[:, l:l + 1], ALU.mult))
                dve.wait_ge(gmax_done, l)
                step(nc.vector.tensor_scalar(bnd[:, l + 1:l + 2], gmax[:, l:l + 1], K[:, l + 1:l + 2], TINY * TO_HALF,
                                             ALU.mult, ALU.max))
                take_scale(l + 1)

            def sum_chunk(j, done):
                for n, part in enumerate((at_hi, at_lo)):
                    dve.wait_ge(deg_dve, done + n)
                    nc.vector.tensor_tensor(S[:, N // 2:N], S[:, N // 2:N], part[:, j, N // 2:N],
                                            ALU.add).then_inc(deg_dve, 1)

            def first_bound():
                dve.wait_ge(gmax_done, 1)
                step(nc.vector.tensor_scalar(K[:, 2:3], cnorm[:, 2:3], zinv[:, 1:2], TO_HALF, ALU.mult, ALU.mult))
                step(nc.vector.tensor_scalar(K[:, 2:3], K[:, 2:3], gmax[:, 1:2], None, ALU.mult))

            def bounds():
                dve.wait_ge(max_done, NC)
                step(nc.vector.tensor_reduce(R[:, :], rowmax[:, :], AX.X, ALU.max))
                step(nc.vector.tensor_scalar(bnd[:, 2:3], R[:, 0:1], K[:, 2:3], TINY * TO_HALF, ALU.mult, ALU.max))
                take_scale(2)
                nc.vector.tensor_scalar(K[:, 3:4], cnorm[:, 3:4], R[:, 0:1], TO_HALF, ALU.mult, ALU.mult)
                nc.vector.tensor_scalar(K[:, 4:5], R[:, :], TO_HALF, None, ALU.mult)
                nc.vector.tensor_scalar(K[:, 6:7], R[:, :], TO_HALF, None, ALU.mult)
                step(nc.vector.tensor_scalar(K[:, 5:6], cnorm[:, 5:6], R[:, 0:1], TO_HALF, ALU.mult, ALU.mult))
                step(nc.vector.tensor_scalar(K[:, 5:6], K[:, 5:6], cnorm[:, 4:5], None, ALU.mult))

            lo_1(0)
            lo_1(1)
            block_scale(0, 0, 0)
            z1_maximum(0)
            lo_1(2)
            lo_1(3)
            low_halves(0, {0: lambda: block_scale(1, 0, 0)})
            low_halves(1, {2: lambda: sum_part(0), 3: lambda: sum_part(1)})
            block_scale(2, 0, 0)
            sum_part(2)
            sum_part(3)
            low_halves(2, {0: lambda: block_scale(3, 0, 0)})
            low_halves(3, {0: lambda: block_scale(4, 0, 0)})
            z1_maximum(1)
            dve.wait_ge(zmax1, 2)
            nc.vector.tensor_tensor(zmax[:, 1:2], zmax[:, 0:1], zmax[:, 7:8], ALU.max).then_inc(zmax_done, 1)
            with dve.Fori(1, G - 1) as g:
                for s in range(CG):
                    low_halves(g * CG + s, {0: lambda: block_scale(g * CG + (s + 1), g - 1, 2 * CG, s + 1)})
                    if s == 1:
                        evacuate(1, g - 1, True)
            steps[0] += 2 * CG * (G - 2)
            for b in range(NC - CG, NC - 1):
                low_halves(b, {0: lambda: block_scale(b + 1, 0, 0)})
                if b == NC - CG + 1:
                    evacuate(1, G - 2, True)
                    first_bound()
            bounds()
            low_halves(NC - 1)
            with dve.Fori(0, G - 1) as it:
                lo(1, it, P)
            evacuate(1, G - 1, True)
            lo(1, G - 1, P)
            dve.wait_ge(z_split, 4 * 2)

            def split(l, it):
                if l == 3:
                    dve.wait_ge(z_act, it + (4 * l + 1))
                    c = bass.ds(it * CG, CG)
                    loop_step(nc.vector.tensor_copy(z_hi[:, 1, c, 0:Q], tmp[:, :, 0:Q]), it, 1, 1)
                    nc.vector.tensor_tensor(z_hi[:, 1, c, Q:P], tmp[:, :, 0:Q], z_hi[:, 1, c, 0:Q],
                                            ALU.subtract).then_inc(z_split, 1)
                else:
                    lo(l, it, Q if l == 2 else P)

            def degrees():
                dve.wait_ge(deg_mm, NC // 2)
                step(nc.vector.tensor_tensor(t16[:, :], work[:, 3, 0:NC], ainv[:, :], ALU.mult))
                nc.vector.tensor_scalar(t16[:, :], t16[:, :], 1.0, None, ALU.add).then_inc(deg_sum, 1)

            def degree_scale():
                dve.wait_ge(deg_pow, 1)
                nc.vector.tensor_reduce(zmax[:, 7:8], dcol[:, :], AX.X, ALU.max).then_inc(zmax_done, 1)
                dve.wait_ge(gmax_done, 6)
                step(nc.vector.tensor_scalar(bnd[:, 6:7], gmax[:, 7:8], LN_BOUND, None, ALU.mult))
                scale_of(7, bnd[:, 6:7], z_scale, 7)
                nc.vector.tensor_scalar(dY[:, :], dcol[:, :], zmul[:, 7:8], None, ALU.mult)
                step(nc.vector.tensor_scalar(dO[:, :], dcol[:, :], zinv[:, 7:8], None, ALU.mult))
                step(nc.vector.tensor_scalar(dO[:, :], dO[:, :], ginv[:, :], winv[:, 1:2], ALU.mult, ALU.mult))

            def late_weights():
                dve.wait_ge(wmax_done, 2)
                step(nc.vector.tensor_scalar(winv[:, :], wall[:, :], TINY, TO_HALF, ALU.max, ALU.mult))
                step(nc.vector.tensor_scalar(winv[:, :].bitcast(I32), winv[:, :].bitcast(I32), EXPONENT, None,
                                             ALU.bitwise_and))
                nc.vector.reciprocal(wmul[:, :], winv[:, :])
                step(nc.vector.tensor_scalar(ginv[:, :], R[:, :], 1.0, 2.0, ALU.add, ALU.mult))
                step(nc.vector.tensor_scalar(ginv[:, :].bitcast(I32), ginv[:, :].bitcast(I32), EXPONENT, None,
                                             ALU.bitwise_and))
                nc.vector.reciprocal(gmul[:, :], ginv[:, :])
                step(nc.vector.tensor_scalar(s6[:, :], zinv[:, 6:7], ginv[:, :], winv[:, 0:1], ALU.mult, ALU.mult))
                nc.vector.tensor_scalar(tab[:, 6, :], ainv[:, :], gmul[:, 0:1], None, ALU.mult)
                for w, mul, halves in ((w6s[:, :], wmul[:, 0:1], w6_halves), (w7s[:, :, :], wmul[:, 1:2], w7_halves)):
                    step(nc.vector.tensor_scalar(w, w, mul, None, ALU.mult))
                    step(nc.vector.tensor_copy(halves[:, 0], w))
                    nc.vector.tensor_tensor(halves[:, 1], w, halves[:, 0], ALU.subtract).then_inc(w_split, 1)

            for l, first, count in ((2, 1, 3), (3, 10, 1), (4, 13, 1)):
                z_maximum(l, Q if l in (3, 4) else P)
                next_scale(l)
                if l == 2:
                    dve.wait_ge(w_late, 32)
                    nc.vector.tensor_reduce(wmax[:, 0:1], w6s[:, :], AX.X, ALU.max, apply_absolute_value=True)
                    nc.vector.tensor_reduce(wmax[:, 1:2], w7s[:, :, :], AX.XY, ALU.max,
                                            apply_absolute_value=True).then_inc(wmax_done, 1)
                    nc.vector.tensor_tensor(S[:, N // 2:N], at_hi[:, 0, N // 2:N], at_lo[:, 0, N // 2:N],
                                            ALU.add).then_inc(deg_dve, 1)
                with dve.Fori(0, G - 1) as it:
                    evacuate(l, it, relu=l == 2)
                    split(l, it)
                    for k in range(count):
                        sum_chunk(it * count + (first + k), it * (2 * count) + (2 * (first + k) - 1))
                evacuate(l, G - 1, relu=l == 2)
                if l == 4:
                    dve.wait_ge(deg_pool, 2 * NC + 1)
                    dve.wait_ge(deg_dve, 2 * NC - 1)
                    nc.vector.tensor_copy(S16[:, 0, :], S[:, :]).then_inc(deg_split, 1)
                    dve.wait_ge(deg_split, 1)
                    nc.vector.tensor_tensor(S16[:, 1, :], S[:, :], S16[:, 0, :], ALU.subtract).then_inc(deg_split, 1)
                split(l, G - 1)
                if l == 3:
                    steps[0] += G
                dve.wait_ge(z_split, 4 * (l + 1))
            z_maximum(5, P)
            next_scale(5)
            for it in range(G):
                evacuate(5, it, relu=True)
                split(5, it)
                if it == 0:
                    degrees()
                if it == 1:
                    late_weights()
                if it == 2:
                    degree_scale()

            def g_low(h):
                nc.vector.tensor_tensor(gT[:, h, 1, :], gsrc[h], gT[:, h, 0, :], ALU.subtract).then_inc(g_split, 1)

            def layer_6(it):
                dve.wait_ge(acc_done, 4 * 5 + it + 1)
                off_scales(pT, it, tab[:, 6, it * CG:(it + 1) * CG]).then_inc(t_ready, 1)
                dve.wait_ge(g_hi, it + 1)
                g_low(0)

            def x1_stats(it):
                c = slice(it * CG, it * CG + CG)
                dve.wait_ge(x_relu, it + 1)
                nc.vector.tensor_tensor(xs[:, c, :], xs[:, c, :], x6, ALU.add).then_inc(x1_done, 1)
                dve.wait_ge(x1_done, it + 1)
                for k in range(CG):
                    last = nc.vector.bn_stats(stat[:, k, :], xs[:, it * CG + k, :])
                step(last)
                for k in range(CG):
                    last = nc.vector.bn_aggr(mv[:, it * CG + k, :], stat[:, k, :])
                step(last)
                nc.vector.tensor_scalar(var[:, c], mv[:, c, 1], EPS, None, ALU.add).then_inc(ln_var, 1)
                dve.wait_ge(ln_pow, it + (G + 1))
                step(nc.vector.tensor_tensor(rstd[:, c], rstd[:, c], dY[:, c], ALU.mult))
                nc.vector.scalar_tensor_tensor(out=nbias[:, c], in0=mv[:, c, 0], scalar=-1.0, in1=rstd[:, c],
                                               op0=ALU.mult, op1=ALU.mult).then_inc(ln_ready, 1)

            def split_y(it):
                c = slice(it * CG, it * CG + CG)
                dve.wait_ge(z_act, it + (4 * 6 + 1))
                nc.vector.tensor_copy(z_hi[:, 0, c, :], tmp[:, :, 0:P])
                step(nc.vector.tensor_copy(y1[:, 0, c, :], tmp[:, :, P:D]))
                nc.vector.tensor_tensor(z_lo[:, 0, c, :], tmp[:, :, 0:P], z_hi[:, 0, c, :], ALU.subtract)
                nc.vector.tensor_tensor(y1[:, 1, c, :], tmp[:, :, P:D], y1[:, 0, c, :],
                                        ALU.subtract).then_inc(z_split, 1)

            layer_6(0)
            x1_stats(0)
            for it in range(1, G):
                layer_6(it)
                split_y(it - 1)
                x1_stats(it)
            split_y(G - 1)

            def a_plus_i(it, h, per=2, parts=1):
                dst, k = gsrc[h], CG // parts
                dve.wait_ge(acc_done, it * 2 + (4 * 6 + h + 1))
                dve.wait_ge(yt_mm, it + 1)
                for q in range(parts):
                    at = slice(q * IT // parts, (q + 1) * IT // parts)
                    t = tab[:, 6, bass.ds(it * CG + q * k, k)].unsqueeze(2).to_broadcast([P, k, P])
                    loop_step(nc.vector.tensor_tensor(
                        dst[:, at].rearrange("p (c n) -> p c n", c=k),
                        acc[:, h * IT + at.start:h * IT + at.stop].rearrange("p (c n) -> p c n", c=k), t, ALU.mult),
                        it, per, h + 1)
                    nc.vector.scalar_tensor_tensor(out=dst[:, at], in0=work[:, h, at], scalar=gmul[:, 0:1],
                                                   in1=dst[:, at], op0=ALU.mult, op1=ALU.add).then_inc(t_ready, 1)

            def result(it):
                for c in range(CG):
                    dve.wait_ge(o_relu, it * CG + (c + 1))
                    k = bass.ds(it * CG + c, 1)
                    nc.vector.tensor_tensor(xs[:, k, :], xs[:, k, :], tmp[:, c:c + 1, :], ALU.add).then_inc(o_done, 1)

            with dve.Fori(0, G - 1) as it:
                for h in range(2):
                    a_plus_i(it, h)
                    dve.wait_ge(g_hi, it * 2 + (4 + h + 1))
                    g_low(h)
                result(it)
            steps[0] += 2 * (G - 1)
            a_plus_i(G - 1, 0, per=0)
            dve.wait_ge(g_hi, 4 + 2 * G - 1)
            g_low(0)
            a_plus_i(G - 1, 1, per=0, parts=2)
            result(G - 1)

        @block.tensor
        def _(pe):
            def keep_warm(n, bank):
                for _ in range(n):
                    nc.tensor.matmul(work[:, bank, 0:P], ones[:, :], ones[:, :], start=True, stop=True)

            pe.wait_ge(consts, 3)
            keep_warm(WARM[0], 0)
            pe.wait_ge(absw_done, 1)
            nc.tensor.matmul(work[:, 3, 0:P], ones[:, :], absw[:, 0:P], start=True, stop=False)
            nc.tensor.matmul(work[:, 3, 0:P], ones[:, :], absw[:, P:2 * P], start=False, stop=True)
            nc.tensor.matmul(work[:, 3, P:3 * P + Q], ones[:, :], absw[:, 2 * P:4 * P + Q], start=True, stop=True)
            nc.tensor.matmul(work[:, 2, 0:P], ones[0:Q, :], absw[0:Q, 4 * P + Q:5 * P + Q], start=True,
                             stop=True).then_inc(norm_mm, 1)

            def ln_transposes(g):
                if g == 0:
                    pe.wait_ge(h_first, 1)
                else:
                    pe.wait_ge(h_done, g)
                if g >= 2:
                    pe.wait_ge(hT_done, g - 1)
                for c in range(CG):
                    for h in range(2):
                        n = (g % 2) * 2 * IT + (2 * c + h) * P
                        last = nc.tensor.transpose(acc[:, n:n + P], h_ln[:, CG * g + c, h * P:(h + 1) * P], eye[:, :])
                last.then_inc(hT_mm, 1)

            def first_z(g):
                pe.wait_ge(hT_done, g + 1)
                if g == 2:
                    pe.wait_ge(norm_read, 1)
                if g == 3:
                    pe.wait_ge(z_scale, 1)
                for c in range(CG):
                    for h in range(2):
                        last = nc.tensor.matmul(work[:, g, c * P:(c + 1) * P], hT[:, CG * g + c, h * P:(h + 1) * P],
                                                W1[:, h, :], start=h == 0, stop=h == 1)
                last.then_inc(z_mm, 1)

            keep_warm(WARM[1], 0)
            ln_transposes(0)
            keep_warm(WARM[2], 0)
            ln_transposes(1)
            first_z(0)
            first_z(1)
            ln_transposes(2)
            ln_transposes(3)
            first_z(2)
            first_z(3)

            def transposes(g, s, q):
                if q == 0:
                    pe.wait_ge(row_in[s], g * 16 + 16)
                for k in range(4):
                    n = (4 * q + k) * P
                    last = nc.tensor.transpose(work[:, q, k * P:(k + 1) * P], ring[:, s, n:n + P], eye[:, :])
                last.then_inc(t_mm, 1)

            for s in range(2):
                for q in range(4):
                    if s == 0:
                        pe.wait_ge(z_split, q + 1)
                    else:
                        pe.wait_ge(a_lo, 4 * (s - 1) + q + 1)
                    transposes(0, s, q)

            def products(l, out_, j, i, first=False, last=False, n=IT):
                if l == 7:
                    zh, zl = z_hi[:, 0, j, :], z_lo[:, 0, j, :]
                elif l == 8:
                    zh, zl = y1[:, 0, j, :], y1[:, 1, j, :]
                else:
                    zh, zl = z_hi[:, (l - 1) % 2, j, :], z_lo[:, (l - 1) % 2, j, :]
                a, b = at_hi[:, j, bass.ds(i, n)], at_lo[:, j, bass.ds(i, n)]
                nc.tensor.matmul(out_, zh, b, start=first, stop=False)
                if l in (3, 4):
                    return nc.tensor.matmul(out_, zh, a, start=False, stop=last)
                nc.tensor.matmul(out_, zl, a, start=False, stop=False)
                return nc.tensor.matmul(out_, zh, a, start=False, stop=last)

            def unit(l, out_, i, slots={}, z_count=None, after=None, js=range(NC)):
                for j in js:
                    if z_count and j % CG == 0:
                        pe.wait_ge(z_split, z_count + j // CG)
                    if j in slots:
                        slots[j]()
                    done = products(l, out_, j, i, first=j == 0, last=j == NC - 1)
                    if after and j >= NC // 2:
                        after(j)
                if js[-1] == NC - 1:
                    done.then_inc(acc_done, 1)

            def bank(it):
                return acc[:, bass.ds(it * IT, IT)]

            def to_nodes(l, it, w, width):
                pe.wait_ge(t_ready, it + (4 * (l - 1) + 1))
                for c in range(CG):
                    last = nc.tensor.matmul(acc[:, bass.ds(it * IT + c * width, width)], zT[:, c * P:(c + 1) * P], w,
                                            start=True, stop=True)
                last.then_inc(z_mm, 1)

            def halves_product(out_, h, c, w, start=True, stop=True):
                hi, lo = gT[:, h, 0, c * P:(c + 1) * P], gT[:, h, 1, c * P:(c + 1) * P]
                nc.tensor.matmul(out_, lo, w[:, 0], start=start, stop=False)
                nc.tensor.matmul(out_, hi, w[:, 1], start=False, stop=False)
                return nc.tensor.matmul(out_, hi, w[:, 0], start=False, stop=stop)

            def small_a(l, it):
                if l == 1:
                    to_nodes(1, it, W2, H)
                elif l == 2:
                    to_nodes(2, it, W3, Q)
                elif l == 3:
                    to_nodes(3, it, eye2[:, :], Q)
                elif l == 4:
                    pe.wait_ge(t_ready, it + (4 * 3 + 1))
                    nc.tensor.matmul(work[:, it, :], W4, pT[:, :], start=True, stop=True).then_inc(mid_mm, 1)
                elif l == 5:
                    pe.wait_ge(t_ready, it + (4 * 4 + 1))
                    pe.wait_ge(z_split, it + 4 * 5)
                    for c in range(CG):
                        last = nc.tensor.transpose(work[:, 0, c * P:(c + 1) * P], zT[:, c * P:(c + 1) * P], eye[:, :])
                    last.then_inc(z_mm, 1)
                elif l == 6:
                    pe.wait_ge(g_split, it + 1)
                    for c in range(CG):
                        last = halves_product(work2[:, c, :], 0, c, w6_halves)
                    last.then_inc(z_mm, 1)

            def small_b(l, it):
                if l == 4:
                    pe.wait_ge(mid_relu, it + 1)
                    for c in range(CG):
                        last = nc.tensor.matmul(acc[:, bass.ds(it * IT + c * P, P)], zT[:, c * P:(c + 1) * P], W5,
                                                start=True, stop=True)
                    last.then_inc(z_mm, 1)

            def first_layer_unit(g, small=True, last=False):
                for h in range(2):
                    for j in range(NC):
                        if j % 4 == 0:
                            pe.wait_ge(a_lo, g * 16 + (8 * h + 5 + j // 4))
                        done = products(1, acc[:, bass.ds(g * IT + h * IT // 2, IT // 2)], j, g * IT + h * IT // 2,
                                        first=j == 0, last=j == NC - 1, n=IT // 2)
                        if j % 2 == 1 and not (last and h == 1):
                            k = 8 * (h + 1) + j // 2
                            pe.wait_ge(a_lo, g * 16 + (k - 3))
                            transposes(g + k // 16, k // 4 % CG, k % 4)
                        if small and h == 1 and j == 2:
                            small_a(1, g - 1)
                done.then_inc(acc_done, 1)

            pe.wait_ge(z_split, 4)
            first_layer_unit(0, small=False)
            with pe.Fori(1, G - 1) as g:
                first_layer_unit(g)
            first_layer_unit(G - 1, last=True)

            def degree_sums(j):
                if j == NC // 2:
                    pe.wait_ge(deg_split, 2)
                for c in (2 * j - NC, 2 * j - NC + 1):
                    for n in range(2):
                        last = nc.tensor.matmul(work[:, 3, c:c + 1], S16[:, n, c * P:(c + 1) * P], ones16[:, :],
                                                start=n == 0, stop=n == 1)
                last.then_inc(deg_mm, 1)

            def slots(l, it, of):
                first = {3: 4, 4: 4, 6: 5 if l == 6 else 2}.get(of, 2)
                return {first: lambda: small_a(l, it), 7: lambda: small_b(l, it)}

            for l in range(2, 7):
                unit(l, bank(0), 0, slots(l - 1, G - 1, l), z_count=4 * (l - 1) + 1,
                     after=degree_sums if l == 5 else None)
                if l < 6:
                    with pe.Fori(1, G) as it:
                        unit(l, bank(it), it * IT, slots(l, it - 1, l))
            pe.wait_ge(w_split, 2)
            unit(6, bank(1), IT, slots(6, 0, 6))
            with pe.Fori(2, G) as it:
                pe.wait_ge(x_relu, it - 1)
                unit(6, bank(it), it * IT, slots(6, it - 1, 6))

            def y_transposed(it):
                for h in range(2):
                    for c in range(CG):
                        j = it * CG + c
                        zh, zl = (z_hi[:, 0, j, :], z_lo[:, 0, j, :]) if h == 0 else (y1[:, 0, j, :], y1[:, 1, j, :])
                        o = work[:, h, c * P:(c + 1) * P]
                        nc.tensor.matmul(o, zl, eye16[:, :], start=True, stop=False)
                        last = nc.tensor.matmul(o, zh, eye16[:, :], start=False, stop=True)
                last.then_inc(yt_mm, 1)

            def last_product(it, h):
                pe.wait_ge(g_split, it * 2 + (4 + 1 + h))
                for c in range(CG):
                    done = halves_product(last4[c], h, c, w7_halves[:, :, h], start=h == 0, stop=h == 1)
                    if h == 1:
                        done.then_inc(gw_mm, 1)

            def very_last_product():
                for c in range(CG):
                    if c % 2 == 0:
                        pe.wait_ge(t_ready, 4 * 6 + 2 * G + c // 2)
                    nc.tensor.matmul(last4[c], zT[:, c * P:(c + 1) * P], w7s[:, 1, :], start=False,
                                     stop=True).then_inc(gw_mm, 1)

            def last_small():
                pe.wait_ge(x_relu, G - 1)
                small_a(6, G - 1)

            def next_first_product(it):
                pe.wait_ge(o_relu, it * CG)
                last_product(it, 0)

            pe.wait_ge(eyes, 3)
            early, late = range(12), range(12, NC)
            unit(7, bank(0), 0, {5: last_small}, z_count=4 * 6 + 1, js=early)
            unit(8, bank(1), 0, js=early)
            pe.wait_ge(x_relu, G)
            y_transposed(0)
            pe.wait_ge(z_split, 4 * 7)
            unit(7, bank(0), 0, js=late)
            unit(8, bank(1), 0, js=late)
            pe.wait_ge(t_ready, 4 * 6 + 1)
            unit(7, bank(0), IT, {2: lambda: last_product(0, 0), 5: lambda: last_product(0, 1)})
            unit(8, bank(1), IT, {2: lambda: y_transposed(1), 7: lambda: next_first_product(1)})
            with pe.Fori(2, G) as it:
                unit(7, bank(0), it * IT, {6: lambda: last_product(it - 1, 1)})
                unit(8, bank(1), it * IT, {2: lambda: y_transposed(it), 7: lambda: next_first_product(it)})
            very_last_product()


_INS = ["x", "adj", "L0_gnn_W1", "L0_gnn_W2", "L0_gnn_W3", "L0_gnn_W4", "L0_gnn_W5", "L0_gnn_W6", "L1_gnn_W"]


def kernel(**inputs):
    import numpy as _np
    import concourse.bacc as _bacc
    from concourse import mybir as _mybir
    from concourse.bass_utils import run_bass_kernel_spmd as _run

    nc = _bacc.Bacc("TRN2", target_bir_lowering=False, num_devices=1)
    arrays, args = {}, []
    for name in _INS:
        a = _np.ascontiguousarray(inputs[name])
        arrays[f"in_{name}"] = a
        args.append(nc.dram_tensor(f"in_{name}", a.shape, _mybir.dt.from_np(a.dtype), kind="ExternalInput").ap())
    out = nc.dram_tensor("out", arrays["in_x"].shape, _mybir.dt.float32, kind="ExternalOutput").ap()
    adjacency_net(nc, *args, out)
    return _run(nc, [arrays], core_ids=[0]).results[0]["out"]
```
